# Optimizing a Trainium2 kernel written in Bass

```python
import numpy as np
import jax
import jax.numpy as jnp

def _softmax(x, axis=-1):
    return jax.nn.softmax(x, axis=axis)
def _gelu(x):
    return jax.nn.gelu(x, approximate=True)
def _silu(x):
    return jax.nn.silu(x)
def _sigmoid(x):
    return jax.nn.sigmoid(x)
def _layernorm(x, axis=-1, eps=1e-5):
    m = jnp.mean(x, axis=axis, keepdims=True)
    v = jnp.var(x, axis=axis, keepdims=True)
    return (x - m) / jnp.sqrt(v + eps)
def _scatter_add(tgt, idx, src, axis=0):
    return tgt.at[idx].add(src)
def _segment_sum(src, seg, n):
    return jax.ops.segment_sum(src, seg, n)

kernel_name = 'mk_conv_seq_d1_conv_nchw512_1da565'

def setup_inputs(seed: int = 0):
    np.random.seed(seed)
    _w = jnp.asarray
    def _rec_inputs():
        import jax
        import jax.numpy as jnp
        _gk = jax.random.key(seed)
        x = 7.22e-05 + 1 * jax.random.normal(jax.random.fold_in(_gk, 1), (16, 512, 32, 32), jnp.float32)
        return x
    x = _rec_inputs()
    def _L0_conv_setup():
        import jax, jax.numpy as jnp
        import numpy as np
        NUM_HEADS = 8
        NUM_GROUPS = 32
        EPS = 1e-05

        def group_norm(x, w, b):
            B, C, H, W = x.shape
            xg = x.reshape(B, NUM_GROUPS, -1)
            mean = xg.mean(axis=-1, keepdims=True)
            var = xg.var(axis=-1, keepdims=True)
            xg = (xg - mean) * jax.lax.rsqrt(var + EPS)
            return xg.reshape(B, C, H, W) * w[None, :, None, None] + b[None, :, None, None]
        key = jax.random.key(seed)
        ks = jax.random.split(key, 3)
        B, C, H, W = (16, 512, 32, 32)
        x = jax.random.normal(ks[0], (B, C, H, W), dtype=jnp.float32)
        norm_w = jnp.ones((C,), jnp.float32)
        norm_b = jnp.zeros((C,), jnp.float32)
        qkv_w = jax.random.normal(ks[1], (3 * C, C), dtype=jnp.float32) * C ** (-0.5)
        qkv_b = jnp.zeros((3 * C,), jnp.float32)
        proj_w = jax.random.normal(ks[2], (C, C), dtype=jnp.float32) * C ** (-0.5)
        proj_b = jnp.zeros((C,), jnp.float32)
        return {'x': x, 'norm_w': norm_w, 'norm_b': norm_b, 'qkv_w': qkv_w, 'qkv_b': qkv_b, 'proj_w': proj_w, 'proj_b': proj_b}
    _L0_conv_all = _L0_conv_setup()
    _L0_conv_in = {k: v for k, v in _L0_conv_all.items() if k in ('norm_w', 'norm_b', 'qkv_w', 'qkv_b', 'proj_w', 'proj_b', )}
    del _L0_conv_all

    return {
        "x": x,
        "L0_conv_norm_w": _L0_conv_in["norm_w"],
        "L0_conv_norm_b": _L0_conv_in["norm_b"],
        "L0_conv_qkv_w": _L0_conv_in["qkv_w"],
        "L0_conv_qkv_b": _L0_conv_in["qkv_b"],
        "L0_conv_proj_w": _L0_conv_in["proj_w"],
        "L0_conv_proj_b": _L0_conv_in["proj_b"],
    }

def reference(x, L0_conv_norm_w, L0_conv_norm_b, L0_conv_qkv_w, L0_conv_qkv_b, L0_conv_proj_w, L0_conv_proj_b):
    import jax
    import jax.numpy as jnp
    def _L0_conv_ref(x, norm_w, norm_b, qkv_w, qkv_b, proj_w, proj_b):
        import jax, jax.numpy as jnp
        import numpy as np
        NUM_HEADS = 8
        NUM_GROUPS = 32
        EPS = 1e-05

        def group_norm(x, w, b):
            B, C, H, W = x.shape
            xg = x.reshape(B, NUM_GROUPS, -1)
            mean = xg.mean(axis=-1, keepdims=True)
            var = xg.var(axis=-1, keepdims=True)
            xg = (xg - mean) * jax.lax.rsqrt(var + EPS)
            return xg.reshape(B, C, H, W) * w[None, :, None, None] + b[None, :, None, None]
        B, C, H, W = x.shape
        nh, hd = (NUM_HEADS, C // NUM_HEADS)
        L = H * W
        h = group_norm(x, norm_w, norm_b)
        qkv = jnp.einsum('oc,bcl->bol', qkv_w, h.reshape(B, C, L)) + qkv_b[None, :, None]
        qkv = qkv.reshape(B, 3, nh, hd, L)
        qkv = jnp.transpose(qkv, (1, 0, 2, 4, 3))
        q, k, v = (qkv[0], qkv[1], qkv[2])
        scale = hd ** (-0.5)
        attn = jax.nn.softmax(jnp.einsum('bnqd,bnkd->bnqk', q, k) * scale, axis=-1)
        h = jnp.einsum('bnqk,bnkd->bnqd', attn, v)
        h = jnp.transpose(h, (0, 1, 3, 2)).reshape(B, C, L)
        h = jnp.einsum('oc,bcl->bol', proj_w, h) + proj_b[None, :, None]
        return h.reshape(B, C, H, W) + x

    def _gn(v, G=32, eps=1e-5):
        B_, C_, H_, W_ = v.shape
        g = v.reshape(B_, G, C_ // G, H_, W_)
        m = jnp.mean(g, axis=(2, 3, 4), keepdims=True)
        s = jnp.var(g, axis=(2, 3, 4), keepdims=True)
        return ((g - m) / jnp.sqrt(s + eps)).reshape(v.shape)

    def _ln_c(v, eps=1e-6):
        m = jnp.mean(v, axis=1, keepdims=True)
        s = jnp.var(v, axis=1, keepdims=True)
        return (v - m) / jnp.sqrt(s + eps)

    def _ln_t(v, eps=1e-5):
        m = jnp.mean(v, axis=-1, keepdims=True)
        s = jnp.var(v, axis=-1, keepdims=True)
        return (v - m) / jnp.sqrt(s + eps)

    def _to_tokens(v):
        B_, C_, H_, W_ = v.shape
        return v.reshape(B_, C_, H_ * W_).transpose(0, 2, 1)
    def _from_tokens(t, like):
        B_, C_, H_, W_ = like.shape
        return t.transpose(0, 2, 1).reshape(B_, C_, H_, W_)

    x = _L0_conv_ref(x, L0_conv_norm_w, L0_conv_norm_b, L0_conv_qkv_w, L0_conv_qkv_b, L0_conv_proj_w, L0_conv_proj_b)
    return x


_drawn_inputs = setup_inputs


def setup_inputs(seed=0):
    import zlib

    import numpy as np

    out = dict(_drawn_inputs(seed))
    spreads = {'L0_conv_norm_w': (1.0, 0.2),
     'L0_conv_norm_b': (0.0, 0.1),
     'L0_conv_qkv_b': (0.0, 0.1),
     'L0_conv_proj_b': (0.0, 0.1)}
    factors = {}
    for name, (base, spread) in spreads.items():
        noise = np.random.default_rng([zlib.crc32(name.encode()), seed]).standard_normal(out[name].shape)
        drawn = base * np.exp(spread * noise) if base else spread * noise
        out[name] = jnp.asarray(drawn.astype(out[name].dtype))
    for name, factor in factors.items():
        out[name] = (out[name] * factor).astype(out[name].dtype)
    return out
```

```python
from contextlib import ExitStack

import numpy as np

import concourse.bass as bass
from concourse import mybir

ALU = mybir.AluOpType
ACT = mybir.ActivationFunctionType
AX_X = mybir.AxisListType.X
F32 = mybir.dt.float32
F16 = mybir.dt.float16

P = 128
GROUPS = 32
EPS = 1e-5
TINY = 1e-30
P_SHIFT = 6.0 * float(np.log(2.0))
M_SCALE = 64.0


def ds(start, size):
    return bass.ds(start, size)


def build_attention_block(nc, x, norm_w, norm_b, qkv_w, qkv_b, proj_w, proj_b, ident_in, group_in, out):
    B, C, H, W = x.shape
    L = H * W
    HEADS = 8
    D = C // HEADS
    CT = C // P
    LT = L // P
    PAIRS = HEADS // 2
    HALF = L // 2
    UNITS = LT
    ROWS = 3 * C + C
    RT = ROWS // P
    SCALE = float(D) ** -0.5
    assert D == 64 and HALF == 512 and CT == 4 and LT == 8

    QKV_USES = 12
    BATCH_ROUNDS = (QKV_USES + CT + HEADS * UNITS) // 2

    def rounds_before_qkv(b):
        return 0 if isinstance(b, int) and b == 0 else BATCH_ROUNDS * b - CT // 2

    def rounds_before_proj(b):
        return BATCH_ROUNDS * b - CT // 2 + (0 if isinstance(b, int) and b == B else QKV_USES // 2)

    def rounds_before_unit(b, head, j):
        return QKV_USES // 2 + BATCH_ROUNDS * b + UNITS // 2 * head + j // 2

    MAX_TILES = {2: (0,), 3: (1,), 4: (2, 3), 5: (4, 5), 6: (6, 7)}

    xv = x.rearrange("b (t p) h w -> b p t (h w)", p=P)
    ov = out.rearrange("b (t p) h w -> b p t (h w)", p=P)
    value_rows = nc.dram_tensor("value_rows", [2, C], F32, kind="Internal").ap()

    with ExitStack() as ctx:

        def sb(name, shape, dt=F32):
            return ctx.enter_context(nc.sbuf_tensor(name, shape, dt))

        def sem(name):
            return ctx.enter_context(nc.semaphore(name))

        w_hi = sb("w_hi", [P, CT, ROWS], F16)
        w_lo = sb("w_lo", [P, CT, ROWS], F16)
        h_hi = sb("h_hi", [P, CT, L], F16)
        h_lo = sb("h_lo", [P, CT, L], F16)
        x_a = sb("x_a", [P, 2, L])
        wide = sb("wide", [P, 2, L])
        qk = sb("qk", [P, 2, 2 * PAIRS, L], F16)
        v_parts = sb("v_parts", [P, HEADS, LT, 2 * D], F16)
        q_a = [sb(f"q_a{i}", [P, L], F16) for i in range(2)]
        q_b = [sb(f"q_b{i}", [P, L], F16) for i in range(2)]
        k_a = [sb(f"k_a{i}", [P, L], F16) for i in range(2)]
        k_b = [sb(f"k_b{i}", [P, L], F16) for i in range(2)]
        v_head = [sb(f"v_head{i}", [P, LT, 2 * D], F16) for i in range(2)]
        prob = [sb(f"prob{i}", [P, 2, HALF]) for i in range(4)]
        p_hi = [sb(f"p_hi{i}", [P, 2, HALF], F16) for i in range(4)]
        p_lo = [sb(f"p_lo{i}", [P, 2, HALF], F16) for i in range(4)]
        psum_keys = [sb(f"psum_keys{i}", [P, HALF]) for i in range(2)]
        o_raw = [sb(f"o_raw{i}", [P, HALF]) for i in range(2)]
        o_sum = sb("o_sum", [P, L])
        o_part = sb("o_part", [P, L])
        denom = sb("denom", [P, L])
        o_hi = sb("o_hi", [P, PAIRS, L], F16)
        o_lo = sb("o_lo", [P, PAIRS, L], F16)
        ident = sb("ident", [P, P])
        ident16 = sb("ident16", [P, P], F16)
        group_mean = sb("group_mean", [P, P])
        ones = sb("ones", [P, P])
        neg_max = [sb(f"neg_max{i}", [P, LT]) for i in range(2)]
        neg_max_scaled = sb("neg_max_scaled", [P, LT])
        neg_max_parts = [sb(f"neg_max_parts{i}", [P, LT, 2], F16) for i in range(2)]
        exp_bias = sb("exp_bias", [P, 1])
        bias_w = sb("bias_w", [P, RT])
        bias_in = sb("bias_in", [P, RT])
        bias = sb("bias", [P, RT])
        row_max = sb("row_max", [P, RT])
        row_scale = sb("row_scale", [P, RT])
        row_inv = sb("row_inv", [P, RT])
        bias_abs = sb("bias_abs", [P, RT])
        qk_scale = sb("qk_scale", [P, 2 * PAIRS])
        qk_bias = sb("qk_bias", [P, 2 * PAIRS])
        stats = sb("stats", [P, CT, 2, 6])
        mean_var = sb("mean_var", [P, CT, 2])
        g_mean = sb("g_mean", [P, CT])
        dev = sb("dev", [P, CT])
        dev2 = sb("dev2", [P, CT])
        spread = sb("spread", [P, CT])
        var_eps = sb("var_eps", [P, CT])
        rstd = sb("rstd", [P, CT])
        minus_half = sb("minus_half", [P, CT])

        w_rows = qk[:].rearrange("p a t l -> p (a t l)").bitcast(F32).rearrange("p (r c) -> p r c", r=RT)
        rows = wide[:].rearrange("p a l -> p (a l)").rearrange("p (r c) -> p r c", r=4)
        NORM_W, NORM_B, V_BIAS, V_SCALE = range(4)

        score = [ctx.enter_context(nc.psum_tensor(f"score{i}", [P, 2, HALF], F32)) for i in range(2)]
        maxes = ctx.enter_context(nc.psum_tensor("maxes", [P, L], F32))
        pv = ctx.enter_context(nc.psum_tensor("pv", [P, HALF], F32))
        sums = ctx.enter_context(nc.psum_tensor("sums", [P, HALF], F32))

        s_setup_in = sem("s_setup_in")
        s_w_in = sem("s_w_in")
        s_consts = sem("s_consts")
        s_setup_v = sem("s_setup_v")
        s_vscale_out = sem("s_vscale_out")
        s_vscale_in = sem("s_vscale_in")
        s_vscale = sem("s_vscale")
        s_wrow = sem("s_wrow")
        s_wt = sem("s_wt")
        s_whi = sem("s_whi")
        s_wlo = sem("s_wlo")
        s_xn = sem("s_xn")
        s_stats = sem("s_stats")
        s_gmean = sem("s_gmean")
        s_spread = sem("s_spread")
        s_gvar = sem("s_gvar")
        s_vareps = sem("s_vareps")
        s_rstd = sem("s_rstd")
        s_xnorm = sem("s_xnorm")
        s_hhi = sem("s_hhi")
        s_hlo = sem("s_hlo")
        s_dve = sem("s_dve")
        s_full = [sem(f"s_full{i}") for i in range(2)]
        s_free = [sem(f"s_free{i}") for i in range(2)]
        s_wide = sem("s_wide")
        s_qkhi = sem("s_qkhi")
        s_qklo = sem("s_qklo")
        s_vhi = sem("s_vhi")
        s_vlo = sem("s_vlo")
        s_res = [sem(f"s_res{i}") for i in range(2)]
        s_y = sem("s_y")
        s_yx = sem("s_yx")
        s_out = [sem(f"s_out{i}") for i in range(2)]
        s_load_a = [sem(f"s_load_a{i}") for i in range(2)]
        s_load_b = [sem(f"s_load_b{i}") for i in range(2)]
        s_max = sem("s_max")
        s_maxed = sem("s_maxed")
        s_mscaled = sem("s_mscaled")
        s_mhi = sem("s_mhi")
        s_mcols = sem("s_mcols")
        s_mrow = sem("s_mrow")
        s_mrows = sem("s_mrows")
        s_exp = sem("s_exp")
        s_phi = sem("s_phi")
        s_plo = sem("s_plo")
        s_pfree = sem("s_pfree")
        s_keysum = sem("s_keysum")
        s_pool = sem("s_pool")
        s_acc = sem("s_acc")
        s_z = sem("s_z")
        s_denom = sem("s_denom")
        s_recip = sem("s_recip")
        s_oraw = sem("s_oraw")
        s_oshift = [sem(f"s_oshift{i}") for i in range(2)]
        s_oadd = sem("s_oadd")
        s_omul = sem("s_omul")
        s_ohi = sem("s_ohi")
        s_olo = sem("s_olo")

        s_passed_sp, s_passed_pe, s_passed_dve = sem("s_passed_sp"), sem("s_passed_pe"), sem("s_passed_dve")

        block = ctx.enter_context(nc.Block())

        def run(eng, qkv, proj, pair, flush):

            def attention(b, norm_next):
                pair(b, 0, True, False, norm_next)
                with eng.Fori(1, PAIRS - 1) as p:
                    pair(b, p, False, False, False)
                pair(b, PAIRS - 1, False, True, norm_next)
                flush(b, norm_next)

            qkv(0)
            attention(0, True)
            with eng.Fori(1, B - 1) as b:
                qkv(b)
                proj(b)
                attention(b, True)
            qkv(B - 1)
            proj(B - 1)
            attention(B - 1, False)
            proj(B)

        @block.sync
        def _(sp):
            def wait_passed(semaphore, value):
                sp.wait_ge(semaphore, value)
                sp.sem_inc(s_passed_sp, 1)

            sp.dma_start(rows[:, NORM_W, :], norm_w.rearrange("(a c) -> a c", a=1).to_broadcast([P, C])).then_inc(s_setup_in, 16)
            sp.dma_start(rows[:, NORM_B, :], norm_b.rearrange("(a c) -> a c", a=1).to_broadcast([P, C])).then_inc(s_setup_in, 16)
            with nc.allow_non_contiguous_dma(reason="biases, once"):
                sp.dma_start(bias_in[:, 0 : RT - CT], qkv_b.rearrange("(t p) -> p t", p=P)).then_inc(s_setup_in, 16)
                sp.dma_start(bias_in[:, RT - CT : RT], proj_b.rearrange("(t p) -> p t", p=P)).then_inc(s_setup_in, 16)
            sp.dma_start(ident[:], ident_in).then_inc(s_setup_in, 16)
            sp.dma_start(group_mean[:], group_in).then_inc(s_setup_in, 16)
            sp.dma_start(w_rows[:, 0 : RT - CT, :], qkv_w.rearrange("(t p) c -> p t c", p=P)).then_inc(s_w_in, 16)
            sp.dma_start(w_rows[:, RT - CT : RT, :], proj_w.rearrange("(t p) c -> p t c", p=P)).then_inc(s_w_in, 16)
            sp.dma_start(x_a[:], xv[0, :, 0:2, :]).then_inc(s_xn, 16)
            sp.wait_ge(s_vscale, 1)
            with nc.allow_non_contiguous_dma(reason="scales and biases, once"):
                sp.dma_start(value_rows[0, :].rearrange("(t p) -> p t", p=P), row_scale[:, 2 * CT : 3 * CT]).then_inc(s_vscale_out, 16)
                sp.dma_start(value_rows[1, :].rearrange("(t p) -> p t", p=P), bias[:, 2 * CT : 3 * CT]).then_inc(s_vscale_out, 16)
            sp.wait_ge(s_vscale_out, 32)
            sp.dma_start(rows[:, V_SCALE, :], value_rows[0:1, :].to_broadcast([P, C])).then_inc(s_vscale_in, 16)
            sp.dma_start(rows[:, V_BIAS, :], value_rows[1:2, :].to_broadcast([P, C])).then_inc(s_vscale_in, 16)
            sp.wait_ge(s_wlo, RT)
            sp.dma_start(wide[:], xv[0, :, 2:4, :]).then_inc(s_xn, 16)

            def load_head(b, p, par):
                r0 = D * par
                hi = lambda t: qk[r0 : r0 + D, 0, ds(t, 1), :].rearrange("p a l -> p (a l)")
                lo = lambda t: qk[r0 : r0 + D, 1, ds(t, 1), :].rearrange("p a l -> p (a l)")
                sp.dma_start(q_a[par][0:D, :], hi(p)).then_inc(s_load_a[par], 16)
                sp.dma_start(q_a[par][D:P, :], lo(p)).then_inc(s_load_a[par], 16)
                sp.dma_start(k_a[par][0:D, :], hi(p + PAIRS)).then_inc(s_load_a[par], 16)
                sp.dma_start(k_a[par][D:P, :], hi(p + PAIRS)).then_inc(s_load_a[par], 16)
                sp.dma_start(q_b[par][0:D, :], hi(p)).then_inc(s_load_b[par], 16)
                sp.dma_start(k_b[par][0:D, :], lo(p + PAIRS)).then_inc(s_load_b[par], 16)
                sp.dma_start(v_head[par][:], v_parts[:, ds(2 * p + par, 1), :, :].rearrange("p a t d -> p (a t) d")).then_inc(s_load_b[par], 16)

            def shift(b, p, par):
                w = 4 * (PAIRS * b + p) + 2 * par
                r0 = D * par
                for qh in range(2):
                    wait_passed(s_oraw, w + qh + 1)
                    if par == 0 and qh == 0:
                        wait_passed(s_olo, PAIRS * b + p + 1)
                        wait_passed(s_ohi, PAIRS * b + p + 1)
                    cols = slice(qh * HALF, (qh + 1) * HALF)
                    sp.dma_start(o_sum[r0 : r0 + D, cols], o_raw[qh][0:D, :]).then_inc(s_oshift[qh], 16)
                    sp.dma_start(o_part[r0 : r0 + D, cols], o_raw[qh][D:P, :]).then_inc(s_oshift[qh], 16)

            def qkv(b):
                wait_passed(s_qklo, 2 + 8 * b + 8)
                wait_passed(s_vlo, 4 * b + 4)
                load_head(b, 0, 0)

            def proj(b):
                for t in range(CT):
                    if t < 2:
                        wait_passed(s_hlo, CT * b + CT if not (isinstance(b, int) and b == B) else CT * B)
                    else:
                        wait_passed(s_yx, CT * (b - 1) + t - 1)
                    sp.dma_start(x_a[:, t % 2, :], xv[ds(b - 1, 1), :, t, :].rearrange("a p l -> p (a l)")).then_inc(s_res[t % 2], 16)
                    if t >= 1:
                        store(b, t - 1)
                store(b, CT - 1)

            def store(b, t):
                wait_passed(s_yx, CT * (b - 1) + t + 1)
                sp.dma_start(ov[ds(b - 1, 1), :, t, :].rearrange("a p l -> p (a l)"), wide[:, t % 2, :]).then_inc(s_out[t % 2], 16)

            def pair(b, p, first, last, norm_next):
                g = HEADS * b + 2 * p
                if first:
                    wait_passed(s_pfree, 4 + UNITS * g)
                else:
                    wait_passed(s_pfree, 4 + UNITS * g)
                load_head(b, p, 1)
                if first and norm_next:
                    if not (isinstance(b, int) and b == 0):
                        wait_passed(s_out[0], 32 * b)
                        wait_passed(s_out[1], 32 * b)
                    sp.dma_start(x_a[:], xv[ds(b + 1, 1), :, 0:2, :].rearrange("a p t l -> p (a t) l")).then_inc(s_xn, 16)
                    sp.dma_start(wide[:], xv[ds(b + 1, 1), :, 2:4, :].rearrange("a p t l -> p (a t) l")).then_inc(s_xn, 16)
                if not first:
                    shift(b, p - 1, 1)
                if not last:
                    wait_passed(s_pfree, 4 + UNITS * (g + 1))
                    load_head(b, p + 1, 0)
                shift(b, p, 0)

            def flush(b, norm_next):
                shift(b, PAIRS - 1, 1)

            run(sp, qkv, proj, pair, flush)
            for i in range(2):
                sp.wait_ge(s_out[i], 32 * B)

        @block.tensor
        def _(pe):
            pe.wait_ge(s_setup_in, 16 * 6)
            for t in range(RT):
                pe.wait_ge(s_wrow, t + 1)
                if t >= 2:
                    pe.wait_ge(s_wlo, t - 1)
                for c in range(CT):
                    mm = pe.transpose(score[t % 2][:, 0, c * P : (c + 1) * P], w_rows[:, t, c * P : (c + 1) * P], ident[:])
                mm.then_inc(s_wt, 1)
            pe.wait_ge(s_wlo, RT)

            def group_products(b):
                pe.wait_ge(s_stats, b + 1)
                pe.matmul(maxes[:, 0:CT], group_mean[:], mean_var[:, :, 0], start=True, stop=True).then_inc(s_gmean, 1)

            def group_spreads(b):
                pe.wait_ge(s_spread, b + 1)
                pe.matmul(maxes[:, CT : 2 * CT], group_mean[:], spread[:], start=True, stop=True).then_inc(s_gvar, 1)

            pe.wait_ge(s_consts, 1)
            group_products(0)
            group_spreads(0)

            def three_products(dst, w0, rhs_hi, rhs_lo):
                for c in range(CT):
                    wh = w_hi[:, c, ds(w0, P)]
                    wl = w_lo[:, c, ds(w0, P)]
                    for n, (w, rhs) in enumerate(((wh, rhs_hi), (wh, rhs_lo), (wl, rhs_hi))):
                        for half in range(2):
                            mm = pe.matmul(dst[:, half, :], w, rhs[:, c, half * HALF : (half + 1) * HALF],
                                           start=(c == 0 and n == 0), stop=(c == CT - 1 and n == 2))
                return mm

            def max_tile(g, par, t):
                if t == 0:
                    pe.wait_ge(s_mrows, g)
                else:
                    pe.wait_ge(s_maxed, LT * g + t)
                for half in range(2):
                    mm = pe.matmul(maxes[:, half * HALF : (half + 1) * HALF], q_a[par][:, t * P : (t + 1) * P],
                                   k_a[par][:, half * HALF : (half + 1) * HALF], start=True, stop=True)
                mm.then_inc(s_max, 1)

            def max_rows(g, par):
                pe.wait_ge(s_mcols, g + 1)
                for t in range(LT):
                    mm = pe.matmul(maxes[0:2, t * P : (t + 1) * P], neg_max_parts[par][:, t, :], ident16[:], start=True, stop=True)
                mm.then_inc(s_mrow, 1)

            def scores(b, p, par, j):
                g = HEADS * b + 2 * p + par
                qh, kp = divmod(j, 4)
                if j == 0:
                    pe.wait_ge(s_load_b[par], 48 * (PAIRS * b + p + 1))
                    pe.wait_ge(s_mrows, g + 1)
                pe.wait_ge(s_free[j % 2], rounds_before_unit(b, 2 * p + par, j) + 1)
                cols = slice(qh * HALF, (qh + 1) * HALF)
                for i in range(2):
                    kt = 2 * kp + i
                    pe.matmul(score[j % 2][:, i, :], k_a[par][:, kt * P : (kt + 1) * P], q_a[par][:, cols], start=True, stop=False)
                    mm = pe.matmul(score[j % 2][:, i, :], k_b[par][0 : D + 2, kt * P : (kt + 1) * P], q_b[par][0 : D + 2, cols],
                                   start=False, stop=True)
                mm.then_inc(s_full[j % 2], 1)

            def values(g, par, j):
                u = UNITS * g + j
                kp = j % 4
                if kp == 0:
                    pe.wait_ge(s_oraw, 2 * g + j // 4)
                pe.wait_ge(s_plo, 4 + u + 1)
                for i in range(2):
                    v = v_head[par][:, 2 * kp + i, :]
                    pe.matmul(pv[:], v, p_hi[j % 4][:, i, :], start=(kp == 0 and i == 0), stop=False)
                    mm = pe.matmul(pv[:], v, p_lo[j % 4][:, i, :], start=False, stop=(kp == 3 and i == 1))
                mm.then_inc(s_pfree, 1)

            def softmax_sums(w, i):
                pe.wait_ge(s_acc, w + 1)
                pe.wait_ge(s_denom, w)
                pe.matmul(sums[:], ones[:], psum_keys[i][:], start=True, stop=True).then_inc(s_z, 1)

            def qkv(b):
                k0 = rounds_before_qkv(b)
                pe.wait_ge(s_hlo, CT * (b + 1))
                pe.sem_inc(s_passed_pe, 1)
                with pe.Fori(0, PAIRS) as p:
                    for i in range(2):
                        pe.wait_ge(s_free[i], k0 + p + 1)
                        three_products(score[i], P * (p + PAIRS * i), h_hi, h_lo).then_inc(s_full[i], 1)
                for i in range(4):
                    pe.wait_ge(s_free[i % 2], k0 + PAIRS + i // 2 + 1)
                    for t in range(2):
                        lt = 2 * i + t
                        cols = slice(lt * P, (lt + 1) * P)
                        for c in range(CT):
                            wh, wl = (w[:, c, 2 * C : 3 * C] for w in (w_hi, w_lo))
                            pe.matmul(score[i % 2][:, t, :], h_hi[:, c, cols], wh, start=(c == 0), stop=False)
                            pe.matmul(score[i % 2][:, t, :], h_hi[:, c, cols], wl, start=False, stop=False)
                            mm = pe.matmul(score[i % 2][:, t, :], h_lo[:, c, cols], wh, start=False, stop=(c == CT - 1))
                    mm.then_inc(s_full[i % 2], 1)

            def proj(b):
                k0 = rounds_before_proj(b)
                pe.wait_ge(s_ohi, 1 + PAIRS * b)
                pe.wait_ge(s_olo, 1 + PAIRS * b)
                pe.sem_inc(s_passed_pe, 1)
                with pe.Fori(0, CT // 2) as t2:
                    for i in range(2):
                        pe.wait_ge(s_free[i], k0 + t2 + 1)
                        three_products(score[i], 3 * C + P * (2 * t2 + i), o_hi, o_lo).then_inc(s_full[i], 1)

            def pair(b, p, first, last, norm_next):
                g = HEADS * b + 2 * p
                if first:
                    pe.wait_ge(s_load_a[0], 64 * (PAIRS * b + 1))
                    for t in range(LT):
                        max_tile(g, 0, t)
                    max_rows(g, 0)
                for par in range(2):
                    before = not (first and par == 0)
                    after = not (last and par == 1)
                    for j in range(UNITS):
                        scores(b, p, par, j)
                        tiles = MAX_TILES.get(j, ()) if after else ()
                        if tiles and tiles[0] == 0:
                            pe.wait_ge(s_load_a[1 - par], 64 * (PAIRS * b + p + par + 1))
                        if tiles:
                            max_tile(g + par + 1, 1 - par, tiles[0])
                        if j >= 2:
                            values(g + par, par, j - 2)
                        elif before:
                            values(g + par - 1, 1 - par, UNITS - 2 + j)
                        for t in tiles[1:]:
                            max_tile(g + par + 1, 1 - par, t)
                        if j == 2 and before:
                            softmax_sums(2 * (g + par) - 1, 1)
                        if j == 3 and norm_next and not after:
                            group_products(b + 1)
                        if j == 5 and norm_next and not after:
                            group_spreads(b + 1)
                    if after:
                        max_rows(g + par + 1, 1 - par)
                    softmax_sums(2 * (g + par), 0)

            def flush(b, norm_next):
                g = HEADS * b + HEADS - 1
                values(g, 1, UNITS - 2)
                values(g, 1, UNITS - 1)
                softmax_sums(2 * g + 1, 1)

            run(pe, qkv, proj, pair, flush)

        @block.scalar
        def _(act):
            for i in range(2):
                act.sem_inc(s_free[i], 1)
            for t in range(RT):
                act.wait_ge(s_wt, t + 1)
                act.activation(w_hi[:, :, t * P : (t + 1) * P], score[t % 2][:, 0, :].rearrange("p (c r) -> p c r", c=CT),
                               ACT.Copy).then_inc(s_whi, 1)

            def normed_high(b, cts):
                for c in cts:
                    act.wait_ge(s_xnorm, CT * b + c + 1)
                    src = x_a if c < 2 else wide
                    act.activation(h_hi[:, c, :], src[:, c % 2, :], ACT.Copy).then_inc(s_hhi, 1)

            normed_high(0, range(CT))

            def qkv(b):
                k0 = rounds_before_qkv(b)
                act.wait_ge(s_hlo, CT * (b + 1))
                with act.Fori(0, PAIRS) as p:
                    for i in range(2):
                        act.wait_ge(s_full[i], k0 + p + 1)
                        act.wait_ge(s_qklo, 2 + 8 * b + 2 * p)
                        tile = p + PAIRS * i
                        act.activation(wide[:, i, :], score[i][:].rearrange("p a l -> p (a l)"), ACT.Identity,
                                       bias=qk_bias[:, ds(tile, 1)], scale=qk_scale[:, ds(tile, 1)]).then_inc(s_wide, 1)
                        act.wait_ge(s_wide, 8 * b + 2 * p + i + 1)
                        act.sem_inc(s_free[i], 1)
                for i in range(4):
                    act.wait_ge(s_full[i % 2], k0 + PAIRS + i // 2 + 1)
                    act.activation(v_parts[:, :, 2 * i : 2 * i + 2, 0:D],
                                   score[i % 2][:].rearrange("p t (n d) -> p n t d", n=HEADS), ACT.Copy).then_inc(s_vhi, 1)

            def proj(b):
                k0 = rounds_before_proj(b)
                batches = B if isinstance(b, int) and b == B else b + 1
                for t in range(CT):
                    act.wait_ge(s_full[t % 2], k0 + t // 2 + 1)
                    if t < 2:
                        act.wait_ge(s_qklo, 2 + 8 * batches)
                    else:
                        act.wait_ge(s_out[t % 2], 32 * (b - 1) + 16)
                    r = 3 * CT + t
                    act.activation(wide[:, t % 2, :], score[t % 2][:].rearrange("p a l -> p (a l)"), ACT.Identity,
                                   bias=bias[:, r : r + 1], scale=row_scale[:, r : r + 1]).then_inc(s_y, 1)
                    act.wait_ge(s_y, CT * (b - 1) + t + 1)
                    act.sem_inc(s_free[t % 2], 1)

            def exponentials(b, p, par, j):
                g = HEADS * b + 2 * p + par
                u = UNITS * g + j
                act.wait_ge(s_full[j % 2], rounds_before_unit(b, 2 * p + par, j) + 1)
                act.wait_ge(s_plo, u + 1)
                act.wait_ge(s_keysum, u + 1)
                act.activation(prob[j % 4][:], score[j % 2][:], ACT.Exp, bias=exp_bias[:, 0:1], scale=SCALE).then_inc(s_exp, 1)
                act.wait_ge(s_exp, u + 1)
                act.sem_inc(s_free[j % 2], 1)
                act.wait_ge(s_pfree, u + 1)
                act.activation(p_hi[j % 4][:], prob[j % 4][:], ACT.Copy).then_inc(s_phi, 1)

            def max_rows(g, par):
                act.wait_ge(s_mrow, g + 1)
                act.activation(q_b[par][D : D + 2, :], maxes[0:2, :], ACT.Copy).then_inc(s_mrows, 1)

            def output(g, qh):
                w = 2 * g + qh
                act.wait_ge(s_pfree, 4 + 4 * (w + 1))
                act.wait_ge(s_oshift[qh], 32 * g + 32)
                act.activation(o_raw[qh][:], pv[:], ACT.Copy).then_inc(s_oraw, 1)

            def denominators(q, par, qh):
                w = 4 * q + 2 * par + qh
                act.wait_ge(s_z, 2 + w + 1)
                if par == 0 and qh == 0:
                    act.wait_ge(s_omul, q + 1)
                r0 = D * par
                act.activation(denom[r0 : r0 + D, qh * HALF : (qh + 1) * HALF], sums[r0 : r0 + D, :], ACT.Copy).then_inc(s_denom, 1)

            def output_high(q, p):
                act.wait_ge(s_omul, 1 + q + 1)
                act.activation(o_hi[:, ds(p, 1), :].rearrange("p a l -> p (a l)"), o_sum[:], ACT.Copy).then_inc(s_ohi, 1)

            def pair(b, p, first, last, norm_next):
                g = HEADS * b + 2 * p
                q = PAIRS * b + p
                if first:
                    max_rows(g, 0)
                for par in range(2):
                    before = not (first and par == 0)
                    after = not (last and par == 1)
                    for j in range(UNITS):
                        exponentials(b, p, par, j)
                        if j == 1 and before:
                            output(g + par - 1, 1)
                        if j == 3 and before:
                            denominators(q - 1 + par, 1 - par, 1)
                        if j == 5:
                            output(g + par, 0)
                        if par == 1 and j == 1 and not first:
                            output_high(q - 1, p - 1)
                    if after:
                        max_rows(g + par + 1, 1 - par)
                    denominators(q, par, 0)

            def flush(b, norm_next):
                g = HEADS * b + HEADS - 1
                q = PAIRS * (b + 1) - 1
                if norm_next:
                    normed_high(b + 1, range(CT))
                output(g, 1)
                denominators(q, 1, 1)
                output_high(q, PAIRS - 1)

            run(act, qkv, proj, pair, flush)

        @block.vector
        def _(dve):
            chain = [0]

            def link(ins):
                chain[0] += 1
                ins.then_inc(s_setup_v, 1)
                dve.wait_ge(s_setup_v, chain[0])

            dve.sem_inc(s_plo, 4)
            dve.sem_inc(s_qklo, 2)
            link(dve.memset(ones[:], 1.0))
            link(dve.memset(exp_bias[:], P_SHIFT))
            link(dve.memset(minus_half[:], -0.5))
            for par in range(2):
                link(dve.memset(k_b[par][D : D + 2, :], M_SCALE))
            dve.wait_ge(s_setup_in, 16 * 6)
            dve.tensor_copy(ident16[:], ident[:]).then_inc(s_consts, 1)
            dve.wait_ge(s_w_in, 32)

            def fold(t, bias_row, scale_row):
                link(dve.tensor_tensor_reduce(w_rows_scratch, w_rows[:, t, :], rows[:, bias_row, :], 1.0, 0.0,
                                              ALU.mult, ALU.add, bias_w[:, t : t + 1]))
                link(dve.tensor_tensor(w_rows[:, t, :], w_rows[:, t, :], rows[:, scale_row, :], ALU.mult))
                link(dve.tensor_reduce(row_max[:, t : t + 1], w_rows[:, t, :], AX_X, ALU.max, apply_absolute_value=True))

            w_rows_scratch = o_part[:, 0:C]

            def scale_rows(t0, t1, with_bias):
                r = slice(t0, t1)
                link(dve.tensor_tensor(bias[:, r], bias_w[:, r], bias_in[:, r], ALU.add))
                if with_bias:
                    link(dve.tensor_scalar(bias_abs[:, r], bias[:, r], -1.0, None, ALU.mult))
                    link(dve.tensor_tensor(bias_abs[:, r], bias_abs[:, r], bias[:, r], ALU.max))
                    link(dve.tensor_tensor(row_max[:, r], row_max[:, r], bias_abs[:, r], ALU.max))
                link(dve.tensor_scalar(row_scale[:, r], row_max[:, r], TINY, None, ALU.max))
                link(dve.reciprocal(row_inv[:, r], row_scale[:, r]))

            def split_rows(t0, t1):
                for t in range(t0, t1):
                    dve.tensor_scalar(w_rows[:, t, :], w_rows[:, t, :], row_inv[:, t : t + 1], None, ALU.mult).then_inc(s_wrow, 1)
                    if t > t0:
                        low_part(t - 1)
                low_part(t1 - 1)

            def low_part(t):
                dve.wait_ge(s_whi, t + 1)
                dve.tensor_tensor(w_lo[:, :, t * P : (t + 1) * P], score[t % 2][:, 0, :].rearrange("p (c r) -> p c r", c=CT),
                                  w_hi[:, :, t * P : (t + 1) * P], ALU.subtract).then_inc(s_wlo, 1)

            for t in range(3 * CT):
                fold(t, NORM_B, NORM_W)
            scale_rows(0, 2 * CT, True)
            scale_rows(2 * CT, 3 * CT, False)
            dve.sem_inc(s_vscale, 1)
            link(dve.tensor_tensor(qk_scale[:, 0:PAIRS], row_scale[:, 0:PAIRS], row_scale[:, PAIRS : 2 * PAIRS], ALU.mult))
            link(dve.memset(qk_scale[:, PAIRS:], 1.0))
            link(dve.tensor_tensor(qk_bias[:, 0:PAIRS], bias[:, 0:PAIRS], row_scale[:, PAIRS : 2 * PAIRS], ALU.mult))
            link(dve.tensor_tensor(qk_bias[:, PAIRS:], bias[:, PAIRS : 2 * PAIRS], row_inv[:, PAIRS : 2 * PAIRS], ALU.mult))
            split_rows(0, 3 * CT)
            dve.wait_ge(s_vscale_in, 32)
            for t in range(3 * CT, RT):
                fold(t, V_BIAS, V_SCALE)
            scale_rows(3 * CT, RT, False)
            split_rows(3 * CT, RT)

            def statistics(b, part):
                src = (x_a, wide)[part]
                dve.wait_ge(s_xn, 32 * b + 16 * (part + 1))
                for i in range(2):
                    for half in range(2):
                        dve.bn_stats(stats[:, 2 * part + i, half, :], src[:, i, half * HALF : (half + 1) * HALF]).then_inc(s_dve, 1)
                dve.wait_ge(s_dve, N_DVE * b + 6 * part + 4)
                dve.sem_inc(s_passed_dve, 1)
                for i in range(2):
                    c = 2 * part + i
                    dve.bn_aggr(mean_var[:, c, :], stats[:, c, :, :].rearrange("p a s -> p (a s)")).then_inc(s_dve, 1)
                if part == 1:
                    dve.wait_ge(s_dve, N_DVE * b + 12)
                    dve.sem_inc(s_stats, 1)

            N_DVE = 15

            def spreads(b):
                dve.wait_ge(s_gmean, b + 1)
                dve.tensor_copy(g_mean[:], maxes[:, 0:CT]).then_inc(s_dve, 1)
                dve.wait_ge(s_dve, N_DVE * b + 13)
                dve.tensor_tensor(dev[:], mean_var[:, :, 0], g_mean[:], ALU.subtract).then_inc(s_dve, 1)
                dve.wait_ge(s_dve, N_DVE * b + 14)
                dve.tensor_tensor(dev2[:], dev[:], dev[:], ALU.mult).then_inc(s_dve, 1)
                dve.wait_ge(s_dve, N_DVE * b + 15)
                dve.tensor_tensor(spread[:], dev2[:], mean_var[:, :, 1], ALU.add).then_inc(s_spread, 1)

            def variance(b):
                dve.wait_ge(s_gvar, b + 1)
                dve.tensor_scalar(var_eps[:], maxes[:, CT : 2 * CT], EPS, None, ALU.add).then_inc(s_vareps, 1)

            def normalise(b):
                dve.wait_ge(s_rstd, b + 1)
                for c in range(CT):
                    t = (x_a if c < 2 else wide)[:, c % 2, :]
                    dve.tensor_scalar(t, t, g_mean[:, c : c + 1], rstd[:, c : c + 1], ALU.subtract, ALU.mult).then_inc(s_xnorm, 1)

            def normed_low(b):
                for c in range(CT):
                    dve.wait_ge(s_hhi, CT * b + c + 1)
                    t = (x_a if c < 2 else wide)[:, c % 2, :]
                    dve.tensor_tensor(h_lo[:, c, :], t, h_hi[:, c, :], ALU.subtract).then_inc(s_hlo, 1)

            statistics(0, 0)
            statistics(0, 1)
            spreads(0)
            variance(0)
            normalise(0)
            normed_low(0)

            def qkv(b):
                with dve.Fori(0, PAIRS) as p:
                    for i in range(2):
                        k = 8 * b + 2 * p + i + 1
                        hi, lo = (qk[:, part, ds(p + PAIRS * i, 1), :].rearrange("p a l -> p (a l)") for part in range(2))
                        dve.wait_ge(s_wide, k)
                        dve.tensor_copy(hi, wide[:, i, :]).then_inc(s_qkhi, 1)
                        dve.wait_ge(s_qkhi, k)
                        dve.tensor_tensor(lo, wide[:, i, :], hi, ALU.subtract).then_inc(s_qklo, 1)
                for i in range(4):
                    dve.wait_ge(s_vhi, 4 * b + i + 1)
                    dve.tensor_tensor(v_parts[:, :, 2 * i : 2 * i + 2, D : 2 * D],
                                      score[i % 2][:].rearrange("p t (n d) -> p n t d", n=HEADS),
                                      v_parts[:, :, 2 * i : 2 * i + 2, 0:D], ALU.subtract).then_inc(s_vlo, 1)
                    dve.wait_ge(s_vlo, 4 * b + i + 1)
                    dve.sem_inc(s_free[i % 2], 1)

            def proj(b):
                for t in range(CT):
                    dve.wait_ge(s_y, CT * (b - 1) + t + 1)
                    dve.wait_ge(s_res[t % 2], 32 * (b - 1) + 16 * (t // 2 + 1))
                    dve.tensor_tensor(wide[:, t % 2, :], wide[:, t % 2, :], x_a[:, t % 2, :], ALU.add).then_inc(s_yx, 1)

            def reduce_max(g, par, t):
                dve.wait_ge(s_max, LT * g + t + 1)
                dve.tensor_reduce(neg_max[par][:, t : t + 1], maxes[:], AX_X, ALU.max, negate=True).then_inc(s_maxed, 1)
                if t == LT - 1:
                    dve.wait_ge(s_maxed, LT * (g + 1))
                    dve.tensor_scalar(neg_max_scaled[:], neg_max[par][:], 1.0 / M_SCALE, None, ALU.mult).then_inc(s_mscaled, 1)
                    dve.wait_ge(s_mscaled, g + 1)
                    dve.tensor_copy(neg_max_parts[par][:, :, 0], neg_max_scaled[:]).then_inc(s_mhi, 1)
                    dve.wait_ge(s_mhi, g + 1)
                    dve.tensor_tensor(neg_max_parts[par][:, :, 1], neg_max_scaled[:], neg_max_parts[par][:, :, 0],
                                      ALU.subtract).then_inc(s_mcols, 1)

            def low_probabilities(u, j):
                dve.wait_ge(s_phi, u + 1)
                dve.wait_ge(s_pfree, u + 1)
                dve.tensor_tensor(p_lo[j % 4][:], prob[j % 4][:], p_hi[j % 4][:], ALU.subtract).then_inc(s_plo, 1)

            def reciprocals(q):
                dve.wait_ge(s_denom, 4 * (q + 1))
                dve.reciprocal(denom[:], denom[:]).then_inc(s_recip, 1)

            def pair(b, p, first, last, norm_next):
                g = HEADS * b + 2 * p
                if first:
                    for t in range(LT):
                        reduce_max(g, 0, t)
                for par in range(2):
                    after = not (last and par == 1)
                    for j in range(UNITS):
                        for t in MAX_TILES.get(j, ()) if after else ():
                            reduce_max(g + par + 1, 1 - par, t)
                        low_probabilities(UNITS * (g + par) + j, j)
                        if par == 0 and not first and j == 6:
                            reciprocals(PAIRS * b + p - 1)
                        if norm_next and not after:
                            if j < 2:
                                statistics(b + 1, j)
                            if j == 4:
                                spreads(b + 1)
                            if j == 6:
                                variance(b + 1)

            def flush(b, norm_next):
                if norm_next:
                    normalise(b + 1)
                    normed_low(b + 1)
                reciprocals(PAIRS * (b + 1) - 1)

            run(dve, qkv, proj, pair, flush)

        @block.gpsimd
        def _(pool):
            pool.sem_inc(s_pfree, 4)
            pool.sem_inc(s_z, 2)
            pool.sem_inc(s_keysum, 4)
            for i in range(2):
                pool.sem_inc(s_oshift[i], 32)
            pool.sem_inc(s_omul, 1)
            pool.sem_inc(s_ohi, 1)
            pool.sem_inc(s_olo, 1)

            def inverse_spread(b):
                pool.wait_ge(s_vareps, b + 1)
                pool.tensor_tensor(rstd[:], var_eps[:], minus_half[:], ALU.pow).then_inc(s_rstd, 1)

            pool.wait_ge(s_setup_v, 3)
            inverse_spread(0)

            ADDS = 7

            def add_keys(u, w, j):
                i, kp = divmod(j, 4)
                acc, pr = psum_keys[i], prob[j % 4]
                pool.wait_ge(s_exp, u + 1)
                if kp == 0:
                    pool.wait_ge(s_z, w + 1)
                    pool.tensor_tensor(acc[:], pr[:, 0, :], pr[:, 1, :], ALU.add).then_inc(s_pool, 1)
                    pool.wait_ge(s_pool, ADDS * w + 1)
                else:
                    for k in range(2):
                        pool.tensor_tensor(acc[:], acc[:], pr[:, k, :], ALU.add).then_inc(s_pool, 1)
                        pool.wait_ge(s_pool, ADDS * w + 2 * kp + k)
                pool.sem_inc(s_keysum, 1)
                if kp == 3:
                    pool.sem_inc(s_acc, 1)

            def merge(q):
                for qh in range(2):
                    pool.wait_ge(s_oshift[qh], 32 + 64 * (q + 1))
                pool.tensor_tensor(o_sum[:], o_sum[:], o_part[:], ALU.add).then_inc(s_oadd, 1)

            def divide(q):
                pool.wait_ge(s_oadd, q + 1)
                pool.wait_ge(s_recip, q + 1)
                pool.tensor_tensor(o_sum[:], o_sum[:], denom[:], ALU.mult).then_inc(s_omul, 1)

            def output_low(q, p):
                pool.wait_ge(s_ohi, 1 + q + 1)
                pool.tensor_tensor(o_lo[:, ds(p, 1), :].rearrange("p a l -> p (a l)"), o_sum[:],
                                   o_hi[:, ds(p, 1), :].rearrange("p a l -> p (a l)"), ALU.subtract).then_inc(s_olo, 1)

            def qkv(b):
                pass

            def proj(b):
                pass

            def pair(b, p, first, last, norm_next):
                g = HEADS * b + 2 * p
                q = PAIRS * b + p
                for par in range(2):
                    after = not (last and par == 1)
                    for j in range(UNITS):
                        add_keys(UNITS * (g + par) + j, 2 * (g + par) + j // 4, j)
                        if not first:
                            if par == 0 and j == 4:
                                merge(q - 1)
                            if par == 0 and j == 7:
                                divide(q - 1)
                            if par == 1 and j == 2:
                                output_low(q - 1, p - 1)
                        if norm_next and not after and j == 7:
                            inverse_spread(b + 1)

            def flush(b, norm_next):
                q = PAIRS * (b + 1) - 1
                merge(q)
                divide(q)
                output_low(q, PAIRS - 1)

            run(pool, qkv, proj, pair, flush)


_INS = ["x", "L0_conv_norm_w", "L0_conv_norm_b", "L0_conv_qkv_w", "L0_conv_qkv_b", "L0_conv_proj_w", "L0_conv_proj_b"]


def kernel(**inputs):
    import numpy as _np
    import concourse.bacc as _bacc
    from concourse import mybir as _mybir
    from concourse.bass_utils import run_bass_kernel_spmd as _run

    nc = _bacc.Bacc("TRN2", target_bir_lowering=False, num_devices=1)
    arrays, args = {}, []
    channels_per_group = inputs["x"].shape[1] // GROUPS
    constants = {
        "identity": _np.eye(P, dtype=_np.float32),
        "group_average": _np.kron(_np.eye(P // channels_per_group), _np.full((channels_per_group,) * 2, 1.0 / channels_per_group)).astype(_np.float32),
    }
    for name in _INS + list(constants):
        a = _np.ascontiguousarray(inputs[name] if name in inputs else constants[name])
        arrays[f"in_{name}"] = a
        args.append(nc.dram_tensor(f"in_{name}", a.shape, _mybir.dt.from_np(a.dtype), kind="ExternalInput").ap())
    y = nc.dram_tensor("out_y", inputs["x"].shape, _mybir.dt.float32, kind="ExternalOutput").ap()
    build_attention_block(nc, *args, y)
    r = _run(nc, [arrays], core_ids=[0])
    return r.results[0]["out_y"]
```

```python
from contextlib import ExitStack

import numpy as np

import concourse.bass as bass
from concourse import mybir

ALU = mybir.AluOpType
ACT = mybir.ActivationFunctionType
AX_X = mybir.AxisListType.X
F32 = mybir.dt.float32
F16 = mybir.dt.float16

P = 128
GROUPS = 32
EPS = 1e-5
TINY = 1e-30
P_SHIFT = 6.0 * float(np.log(2.0))
M_SCALE = 64.0
INV_SCALE = 4096.0


def ds(start, size):
    return bass.ds(start, size)


def build_attention_block(nc, x, norm_w, norm_b, qkv_w, qkv_b, proj_w, proj_b, ident_in, group_in, out):
    B, C, H, W = x.shape
    L = H * W
    HEADS = 8
    D = C // HEADS
    CT = C // P
    LT = L // P
    PAIRS = HEADS // 2
    T = B * PAIRS
    HALF = L // 2
    UNITS = LT
    ROWS = 3 * C + C
    RT = ROWS // P
    SCALE = float(D) ** -0.5
    assert D == 64 and HALF == 512 and CT == 4 and LT == 8 and PAIRS == CT

    Q0, Q1, K0, K1, V0, V1, O0, O1 = range(8)

    def side_uses(t):
        return 6 + 6 * t if isinstance(t, int) and t < PAIRS else 8 * t - 2

    EARLY_TILE = {3: 1, 4: 3, 5: 5, 6: 7}
    LATE_TILE = {2: 0, 3: 2, 4: 4, 5: 6}

    x_tiles = x.rearrange("b (t p) h w -> (b t) p (h w)", p=P)
    out_tiles = out.rearrange("b (t p) h w -> (b t) p (h w)", p=P)
    value_rows = nc.dram_tensor("value_rows", [2, C], F32, kind="Internal").ap()

    with ExitStack() as ctx:

        def sb(name, shape, dt=F32):
            return ctx.enter_context(nc.sbuf_tensor(name, shape, dt))

        def sem(name):
            return ctx.enter_context(nc.semaphore(name))

        def sems(name):
            return [sem(f"{name}{i}") for i in range(2)]

        w_hi = sb("w_hi", [P, CT, ROWS], F16)
        w_lo = sb("w_lo", [P, CT, ROWS], F16)
        h_hi = sb("h_hi", [P, 2 * CT, L], F16)
        h_lo = sb("h_lo", [P, 2 * CT, L], F16)
        o_hi = sb("o_hi", [P, 2 * PAIRS, L], F16)
        o_lo = sb("o_lo", [P, 2 * PAIRS, L], F16)
        x_norm = sb("x_norm", [P, L])
        x_res = [sb(f"x_res{i}", [P, HALF]) for i in range(2)]
        y_tile = [sb(f"y_tile{i}", [P, HALF]) for i in range(2)]
        qk_full = [sb(f"qk_full{i}", [P, HALF]) for i in range(2)]
        qk = sb("qk", [P, 2, 2, L], F16)
        v_new = sb("v_new", [P, 2, LT, 2 * D], F16)
        q_a = [sb(f"q_a{i}", [P, L], F16) for i in range(2)]
        q_b = [sb(f"q_b{i}", [P, L], F16) for i in range(2)]
        k_a = [sb(f"k_a{i}", [P, L], F16) for i in range(2)]
        k_b = [sb(f"k_b{i}", [P, L], F16) for i in range(2)]
        v_head = [sb(f"v_head{i}", [P, LT, 2 * D], F16) for i in range(2)]
        prob_all = sb("prob_all", [P, 4, 2, HALF])
        p_parts = sb("p_parts", [P, 2, 4, 2, HALF], F16)
        prob = [prob_all[:, i] for i in range(4)]
        p_hi = [p_parts[:, 0, i] for i in range(4)]
        p_lo = [p_parts[:, 1, i] for i in range(4)]
        key_sums = [sb(f"key_sums{i}", [P, HALF]) for i in range(2)]
        key_parts = [sb(f"key_parts{i}", [P, 2, HALF], F16) for i in range(2)]
        o_raw = [sb(f"o_raw{i}", [P, HALF]) for i in range(2)]
        o_pair = sb("o_pair", [P, 2, L])
        o_sum, o_part = o_pair[:, 0, :], o_pair[:, 1, :]
        denom = sb("denom", [P, L])
        ident = sb("ident", [P, P])
        ident16 = sb("ident16", [P, P], F16)
        group_mean = sb("group_mean", [P, P])
        ones = sb("ones", [P, 1], F16)
        neg_max = [sb(f"neg_max{i}", [P, LT]) for i in range(2)]
        neg_max_scaled = sb("neg_max_scaled", [P, LT])
        neg_max_parts = [sb(f"neg_max_parts{i}", [P, LT, 2], F16) for i in range(2)]
        inv = sb("inv", [P, LT])
        inv_scaled = sb("inv_scaled", [P, LT])
        inv_parts = sb("inv_parts", [P, 2, LT], F16)
        exp_bias = sb("exp_bias", [P, 1])
        bias_w = sb("bias_w", [P, RT])
        bias_in = sb("bias_in", [P, RT])
        bias = sb("bias", [P, RT])
        row_max = sb("row_max", [P, RT])
        row_scale = sb("row_scale", [P, RT])
        row_inv = sb("row_inv", [P, RT])
        bias_abs = sb("bias_abs", [P, RT])
        qk_scale = sb("qk_scale", [P, 2 * PAIRS])
        qk_bias = sb("qk_bias", [P, 2 * PAIRS])
        stats = sb("stats", [P, 2, 6])
        mean_var = sb("mean_var", [P, 2])
        g_mean = sb("g_mean", [P, 1])
        dev = sb("dev", [P, 1])
        dev2 = sb("dev2", [P, 1])
        spread = sb("spread", [P, 1])
        var_eps = sb("var_eps", [P, 1])
        rstd = sb("rstd", [P, 1])
        minus_half = sb("minus_half", [P, 1])

        row_homes = (prob_all[:].rearrange("p a b l -> p (a b l)"),
                     p_parts[:].rearrange("p a b c l -> p (a b c l)").bitcast(F32))

        def w_row(t):
            return row_homes[t // 8][:, (t % 8) * C : (t % 8 + 1) * C]

        rows = o_pair[:].rearrange("p a l -> p (a l)").rearrange("p (r c) -> p r c", r=4)
        NORM_W, NORM_B, V_BIAS, V_SCALE = range(4)

        score = [ctx.enter_context(nc.psum_tensor(f"score{i}", [P, 2, HALF], F32)) for i in range(2)]
        maxes = ctx.enter_context(nc.psum_tensor("maxes", [P, L], F32))
        pv = ctx.enter_context(nc.psum_tensor("pv", [P, HALF], F32))
        side = ctx.enter_context(nc.psum_tensor("side", [P, HALF], F32))

        s_setup_in = sem("s_setup_in")
        s_w_in = sem("s_w_in")
        s_consts = sem("s_consts")
        s_setup_v = sem("s_setup_v")
        s_vscale = sem("s_vscale")
        s_vscale_out = sem("s_vscale_out")
        s_vscale_in = sem("s_vscale_in")
        s_wrow = sem("s_wrow")
        s_wt = sem("s_wt")
        s_whi = sem("s_whi")
        s_wlo = sem("s_wlo")
        s_xn = sem("s_xn")
        s_bn = sem("s_bn")
        s_stats = sem("s_stats")
        s_gmean = sem("s_gmean")
        s_dve = sem("s_dve")
        s_spread = sem("s_spread")
        s_gvar = sem("s_gvar")
        s_vareps = sem("s_vareps")
        s_rstd = sem("s_rstd")
        s_xnorm = sem("s_xnorm")
        s_hhi = sem("s_hhi")
        s_hlo = sem("s_hlo")
        s_side_full = sem("s_side_full")
        s_side_free = sem("s_side_free")
        s_qkfull = sem("s_qkfull")
        s_qkhi = sem("s_qkhi")
        s_qklo = sem("s_qklo")
        s_vhi = sem("s_vhi")
        s_vlo = sem("s_vlo")
        s_res = sems("s_res")
        s_y = sem("s_y")
        s_yx = sem("s_yx")
        s_out = sems("s_out")
        s_load_a = sems("s_load_a")
        s_load_b = sems("s_load_b")
        s_load_v = sems("s_load_v")
        s_full = sems("s_full")
        s_free = sems("s_free")
        s_max = sem("s_max")
        s_maxed = sem("s_maxed")
        s_mscaled = sem("s_mscaled")
        s_mhi = sem("s_mhi")
        s_mcols = sem("s_mcols")
        s_mrow = sem("s_mrow")
        s_mrows = sem("s_mrows")
        s_exp = sem("s_exp")
        s_phi = sem("s_phi")
        s_plo = sem("s_plo")
        s_pfree = sem("s_pfree")
        s_keysum = sem("s_keysum")
        s_pool = sem("s_pool")
        s_acc = sem("s_acc")
        s_keyhi = sem("s_keyhi")
        s_keylo = sem("s_keylo")
        s_z = sem("s_z")
        s_inv = sem("s_inv")
        s_inv_scaled = sem("s_inv_scaled")
        s_invhi = sem("s_invhi")
        s_invparts = sem("s_invparts")
        s_invrow = sem("s_invrow")
        s_denom = sem("s_denom")
        s_oraw = sem("s_oraw")
        s_oshift = sems("s_oshift")
        s_oadd = sem("s_oadd")
        s_omul = sem("s_omul")
        s_ohi = sem("s_ohi")
        s_olo = sem("s_olo")
        s_passed = {name: sem(f"s_passed_{name}") for name in ("sp", "pe", "act", "dve")}

        block = ctx.enter_context(nc.Block())

        def steps(eng, pair, flush):
            pair(0, before=False, after=True, qkv=True, norm=True, proj=False)
            for t in range(1, PAIRS):
                pair(t, before=True, after=True, qkv=True, norm=True, proj=False)
            with eng.Fori(PAIRS, T - PAIRS - 1) as t:
                pair(t, before=True, after=True, qkv=True, norm=True, proj=True)
            with eng.Fori(T - PAIRS - 1, T - 1) as t:
                pair(t, before=True, after=True, qkv=True, norm=False, proj=True)
            pair(T - 1, before=True, after=False, qkv=False, norm=False, proj=True)
            flush()

        def proj_uses(t, after_qkv):
            return side_uses(t) + (6 if after_qkv else 0)

        LAST_USES = side_uses(T - 1) + 2

        @block.sync
        def _(sp):
            def wait_passed(semaphore, value):
                sp.wait_ge(semaphore, value)
                sp.sem_inc(s_passed["sp"], 1)

            sp.dma_start(rows[:, NORM_W, :], norm_w.rearrange("(a c) -> a c", a=1).to_broadcast([P, C])).then_inc(s_setup_in, 16)
            sp.dma_start(rows[:, NORM_B, :], norm_b.rearrange("(a c) -> a c", a=1).to_broadcast([P, C])).then_inc(s_setup_in, 16)
            with nc.allow_non_contiguous_dma(reason="biases, once"):
                sp.dma_start(bias_in[:, 0 : RT - CT], qkv_b.rearrange("(t p) -> p t", p=P)).then_inc(s_setup_in, 16)
                sp.dma_start(bias_in[:, RT - CT : RT], proj_b.rearrange("(t p) -> p t", p=P)).then_inc(s_setup_in, 16)
            sp.dma_start(ident[:], ident_in).then_inc(s_setup_in, 16)
            sp.dma_start(group_mean[:], group_in).then_inc(s_setup_in, 16)
            qkv_rows = qkv_w.rearrange("(t p) c -> p t c", p=P)
            sp.dma_start(row_homes[0].rearrange("p (t c) -> p t c", c=C), qkv_rows[:, 0:8, :]).then_inc(s_w_in, 16)
            sp.dma_start(row_homes[1][:, 0 : 4 * C].rearrange("p (t c) -> p t c", c=C), qkv_rows[:, 8:12, :]).then_inc(s_w_in, 16)
            sp.dma_start(row_homes[1][:, 4 * C : 8 * C].rearrange("p (t c) -> p t c", c=C),
                         proj_w.rearrange("(t p) c -> p t c", p=P)).then_inc(s_w_in, 16)
            sp.wait_ge(s_vscale, 1)
            with nc.allow_non_contiguous_dma(reason="scales and biases, once"):
                sp.dma_start(value_rows[0, :].rearrange("(t p) -> p t", p=P), row_scale[:, 2 * CT : 3 * CT]).then_inc(s_vscale_out, 16)
                sp.dma_start(value_rows[1, :].rearrange("(t p) -> p t", p=P), bias[:, 2 * CT : 3 * CT]).then_inc(s_vscale_out, 16)
            sp.wait_ge(s_vscale_out, 32)
            sp.dma_start(rows[:, V_SCALE, :], value_rows[0:1, :].to_broadcast([P, C])).then_inc(s_vscale_in, 16)
            sp.dma_start(rows[:, V_BIAS, :], value_rows[1:2, :].to_broadcast([P, C])).then_inc(s_vscale_in, 16)

            def load_x(m):
                sp.dma_start(x_norm[:], x_tiles[ds(m, 1), :, :].rearrange("a p l -> p (a l)")).then_inc(s_xn, 16)

            for m in range(CT + 1):
                if m:
                    wait_passed(s_hlo, m)
                load_x(m)

            def load_scores(par):
                r = slice(D * par, D * par + D)
                sp.dma_start(q_a[par][0:D, :], qk[r, 0, 0, :]).then_inc(s_load_a[par], 16)
                sp.dma_start(k_a[par][0:D, :], qk[r, 0, 1, :]).then_inc(s_load_a[par], 16)
                sp.dma_start(q_a[par][D:P, :], qk[r, 1, 0, :]).then_inc(s_load_a[par], 16)
                sp.dma_start(k_a[par][D:P, :], qk[r, 0, 1, :]).then_inc(s_load_a[par], 16)
                sp.dma_start(q_b[par][0:D, :], qk[r, 0, 0, :]).then_inc(s_load_b[par], 16)
                sp.dma_start(k_b[par][0:D, :], qk[r, 1, 1, :]).then_inc(s_load_b[par], 16)

            def load_values(par):
                sp.dma_start(v_head[par][:], v_new[:, par, :, :]).then_inc(s_load_v[par], 16)

            def shift(g, par):
                r = slice(D * par, D * par + D)
                for qh in range(2):
                    wait_passed(s_oraw, 2 * g + qh + 1)
                    cols = slice(qh * HALF, (qh + 1) * HALF)
                    sp.dma_start(o_sum[r, cols], o_raw[qh][0:D, :]).then_inc(s_oshift[qh], 16)
                    sp.dma_start(o_part[r, cols], o_raw[qh][D:P, :]).then_inc(s_oshift[qh], 16)

            def load_residual(t):
                wait_passed(s_yx, 2 + 2 * (t - PAIRS))
                for qh in range(2):
                    sp.dma_start(x_res[qh][:], x_tiles[ds(t - PAIRS, 1), :, qh * HALF : (qh + 1) * HALF].rearrange("a p l -> p (a l)")).then_inc(s_res[qh], 16)

            def store(t):
                for qh in range(2):
                    wait_passed(s_yx, 2 + 2 * (t - PAIRS) + qh + 1)
                    sp.dma_start(out_tiles[ds(t - PAIRS, 1), :, qh * HALF : (qh + 1) * HALF].rearrange("a p l -> p (a l)"), y_tile[qh][:]).then_inc(s_out[qh], 16)

            wait_passed(s_qklo, 2 + 4)
            load_scores(0)
            load_scores(1)
            wait_passed(s_vlo, 2)
            load_values(0)

            def pair(t, before, after, qkv, norm, proj):
                g = 2 * t
                if norm:
                    wait_passed(s_hlo, t + CT + 1)
                    load_x(t + CT + 1)
                if before:
                    wait_passed(s_pfree, 4 + UNITS * g)
                load_values(1)
                if proj:
                    load_residual(t)
                if before:
                    shift(g - 1, 1)
                if after:
                    wait_passed(s_qklo, 2 + 4 * (t + 2))
                    wait_passed(s_exp, UNITS * (g + 1))
                    load_scores(0)
                wait_passed(s_olo, t + 1)
                wait_passed(s_ohi, t + 1)
                shift(g, 0)
                if after:
                    wait_passed(s_vlo, 2 * (t + 2))
                    wait_passed(s_pfree, 4 + UNITS * (g + 1))
                    load_values(0)
                    wait_passed(s_exp, UNITS * (g + 2))
                    load_scores(1)
                if proj:
                    store(t)

            def flush():
                shift(HEADS * B - 1, 1)
                with sp.Fori(T, T + PAIRS) as t:
                    load_residual(t)
                    store(t)

            steps(sp, pair, flush)
            for i in range(2):
                sp.wait_ge(s_out[i], 16 + 16 * T)

        @block.tensor
        def _(pe):
            pe.wait_ge(s_setup_in, 16 * 6)
            for t in range(RT):
                pe.wait_ge(s_wrow, t + 1)
                if t >= 2:
                    pe.wait_ge(s_wlo, t - 1)
                for c in range(CT):
                    mm = pe.transpose(score[t % 2][:, 0, c * P : (c + 1) * P], w_row(t)[:, c * P : (c + 1) * P], ident[:])
                mm.then_inc(s_wt, 1)
            pe.wait_ge(s_wlo, RT)
            pe.wait_ge(s_consts, 1)

            def group_product(m):
                pe.wait_ge(s_stats, m + 1)
                pe.matmul(maxes[:, 16:17], group_mean[:], mean_var[:, 0:1], start=True, stop=True).then_inc(s_gmean, 1)

            def group_spread(m):
                pe.wait_ge(s_spread, m + 1)
                pe.matmul(maxes[:, 17:18], group_mean[:], spread[:], start=True, stop=True).then_inc(s_gvar, 1)

            for m in range(CT + 1):
                group_product(m)
                group_spread(m)
            pe.wait_ge(s_vareps, CT + 1)

            def half_of_products(w0, rhs_hi, rhs_lo, slot, qh, part):
                cols = slice(qh * HALF, (qh + 1) * HALF)
                for c in range(2 * part, 2 * part + 2):
                    r_hi, r_lo = (r[:, ds(slot + c, 1), cols].rearrange("p a l -> p (a l)") for r in (rhs_hi, rhs_lo))
                    pe.matmul(side[:], w_hi[:, c, ds(w0, P)], r_hi, start=(c == 0), stop=False)
                    pe.matmul(side[:], w_hi[:, c, ds(w0, P)], r_lo, start=False, stop=False)
                    mm = pe.matmul(side[:], w_lo[:, c, ds(w0, P)], r_hi, start=False, stop=(c == CT - 1))
                return mm

            def value_products(pair_of, slot, vh, part):
                for lt in range(4 * vh + 2 * part, 4 * vh + 2 * part + 2):
                    dst = side[:, (lt % 4) * P : (lt % 4 + 1) * P]
                    for c in range(CT):
                        hh, hl = (h[:, ds(slot + c, 1), lt * P : (lt + 1) * P].rearrange("p a l -> p (a l)") for h in (h_hi, h_lo))
                        wh, wl = (w[:, c, ds(2 * C + P * pair_of, P)] for w in (w_hi, w_lo))
                        pe.matmul(dst, hh, wh, start=(c == 0), stop=False)
                        pe.matmul(dst, hh, wl, start=False, stop=False)
                        mm = pe.matmul(dst, hl, wh, start=False, stop=(c == CT - 1))
                return mm

            def side_product(uses, target, group, part):
                if part == 0:
                    pe.wait_ge(s_side_free, uses + group + 1)
                slot = CT * ((target // CT) % 2) if isinstance(target, int) else CT * ((target >> 2) & 1)
                of = target % CT if isinstance(target, int) else target & 3
                if group in (V0, V1):
                    mm = value_products(of, slot, group - V0, part)
                elif group in (O0, O1):
                    mm = half_of_products(3 * C + P * of, o_hi, o_lo, slot, group - O0, part)
                else:
                    mm = half_of_products((C if group >= K0 else 0) + P * of, h_hi, h_lo, slot, group % 2, part)
                if part == 1:
                    mm.then_inc(s_side_full, 1)

            def max_tile(g, par, t):
                if t == 0:
                    pe.wait_ge(s_load_a[par], 64 * (g // 2 + 1) if isinstance(g, int) else 64 * (g >> 1) + 64)
                else:
                    pe.wait_ge(s_maxed, LT * g + t)
                for half in range(2):
                    mm = pe.matmul(maxes[:, half * HALF : (half + 1) * HALF], q_a[par][:, t * P : (t + 1) * P],
                                   k_a[par][:, half * HALF : (half + 1) * HALF], start=True, stop=True)
                mm.then_inc(s_max, 1)

            def max_rows(g, par):
                pe.wait_ge(s_mcols, g + 1)
                for t in range(LT):
                    mm = pe.matmul(maxes[0:2, t * P : (t + 1) * P], neg_max_parts[par][:, t, :], ident16[:], start=True, stop=True)
                mm.then_inc(s_mrow, 1)

            def scores(t, par, j):
                g = 2 * t + par
                qh, kp = divmod(j, 4)
                if j == 0:
                    pe.wait_ge(s_load_b[par], 32 * (t + 1))
                    pe.wait_ge(s_mrows, g + 1)
                pe.wait_ge(s_free[j % 2], UNITS // 2 * g + j // 2 + 1)
                cols = slice(qh * HALF, (qh + 1) * HALF)
                for i in range(2):
                    keys = slice((2 * kp + i) * P, (2 * kp + i + 1) * P)
                    pe.matmul(score[j % 2][:, i, :], k_a[par][:, keys], q_a[par][:, cols], start=True, stop=False)
                    mm = pe.matmul(score[j % 2][:, i, :], k_b[par][0 : D + 2, keys], q_b[par][0 : D + 2, cols], start=False, stop=True)
                mm.then_inc(s_full[j % 2], 1)

            def values(g, par, j):
                kp = j % 4
                if j == 0:
                    pe.wait_ge(s_load_v[par], 16 * (g // 2 + 1) if isinstance(g, int) else 16 * (g >> 1) + 16)
                if kp == 0 and not (isinstance(g, int) and g == 0 and j == 0):
                    pe.wait_ge(s_oraw, 2 * g + j // 4)
                pe.wait_ge(s_plo, 4 + UNITS * g + j + 1)
                for i in range(2):
                    v = v_head[par][:, 2 * kp + i, :]
                    pe.matmul(pv[:], v, p_hi[j % 4][:, i, :], start=(kp == 0 and i == 0), stop=False)
                    mm = pe.matmul(pv[:], v, p_lo[j % 4][:, i, :], start=False, stop=(kp == 3 and i == 1))
                mm.then_inc(s_pfree, 1)

            def softmax_sums(g):
                pe.wait_ge(s_keylo, 2 + 2 * (g + 1))
                for t in range(LT):
                    for part in range(2):
                        mm = pe.matmul(maxes[:, 8 + t : 9 + t], key_parts[t // 4][:, part, (t % 4) * P : (t % 4 + 1) * P], ones[:],
                                       start=(part == 0), stop=(part == 1))
                mm.then_inc(s_z, 1)

            def inverse_rows(g):
                pe.wait_ge(s_invparts, g + 1)
                for t in range(LT):
                    for part in range(2):
                        mm = pe.matmul(maxes[:, t * P : (t + 1) * P], inv_parts[:, part, t : t + 1].to_broadcast([P, P]), ident16[:],
                                       start=(part == 0), stop=(part == 1))
                mm.then_inc(s_invrow, 1)

            pe.wait_ge(s_hlo, CT)
            for group in range(6):
                for part in range(2):
                    side_product(0, 0, group, part)
            pe.wait_ge(s_hlo, CT + 1)
            for t in range(LT):
                max_tile(0, 0, t)
            max_rows(0, 0)

            def pair(t, before, after, qkv, norm, proj):
                for par in range(2):
                    g = 2 * t + par
                    previous = before or par == 1
                    following = after or par == 0
                    for j in range(UNITS):
                        if j == 0:
                            if previous:
                                values(g - 1, 1 - par, UNITS - 2)
                            scores(t, par, j)
                            if norm and par == 1:
                                group_product(t + CT + 1)
                        else:
                            if norm and par == 1 and j == 1:
                                group_spread(t + CT + 1)
                            scores(t, par, j)
                            if j >= 2:
                                values(g, par, j - 2)
                            elif previous:
                                values(g - 1, 1 - par, UNITS - 1)
                        if j == 2 and previous:
                            inverse_rows(g - 1)
                        if j == UNITS - 1 and following:
                            max_rows(g + 1, 1 - par)
                        group = (UNITS * par + j) // 2
                        if following and j in EARLY_TILE:
                            max_tile(g + 1, 1 - par, EARLY_TILE[j])
                        if group in (Q0, V0) and j == 0 and qkv:
                            pe.wait_ge(s_hlo, CT * ((t + 1) >> 2) + CT)
                            pe.sem_inc(s_passed["pe"], 1)
                        if group < O0 and qkv:
                            side_product(side_uses(t), t + 1, group, j % 2)
                        if group >= O0 and proj:
                            if group == O0 and j % 2 == 0:
                                pe.wait_ge(s_olo, 1 + t)
                                pe.wait_ge(s_ohi, 1 + t)
                            side_projection(t, group, j % 2, qkv)
                        if following and j in LATE_TILE:
                            if LATE_TILE[j] == 0 and previous:
                                pe.wait_ge(s_denom, g)
                            max_tile(g + 1, 1 - par, LATE_TILE[j])
                        if j == 1 and previous:
                            if norm and par == 1:
                                pe.wait_ge(s_vareps, t + CT + 2)
                            softmax_sums(g - 1)

            def side_projection(t, group, part, after_qkv):
                uses = proj_uses(t, after_qkv) - O0
                side_product(uses, t - PAIRS, group, part)

            def flush():
                g = HEADS * B - 1
                for j in range(2):
                    values(g, 1, UNITS - 2 + j)
                softmax_sums(g)
                inverse_rows(g)
                pe.wait_ge(s_olo, 1 + T)
                pe.wait_ge(s_ohi, 1 + T)
                with pe.Fori(0, CT) as c:
                    for group in (O0, O1):
                        for part in range(2):
                            side_product(LAST_USES + 2 * c - O0, T - PAIRS + c, group, part)

            steps(pe, pair, flush)

        @block.scalar
        def _(act):
            for i in range(2):
                act.sem_inc(s_free[i], 1)
            act.sem_inc(s_side_free, 1)
            for t in range(RT):
                act.wait_ge(s_wt, t + 1)
                act.activation(w_hi[:, :, t * P : (t + 1) * P], score[t % 2][:, 0, :].rearrange("p (c r) -> p c r", c=CT),
                               ACT.Copy).then_inc(s_whi, 1)

            def slot_of(m):
                return ds(m % (2 * CT) if isinstance(m, int) else m & (2 * CT - 1), 1)

            def normed_high(m):
                act.wait_ge(s_xnorm, m + 1)
                act.sem_inc(s_passed["act"], 1)
                act.activation(h_hi[:, slot_of(m), :].rearrange("p a l -> p (a l)"), x_norm[:], ACT.Copy).then_inc(s_hhi, 1)

            for m in range(CT + 1):
                normed_high(m)

            def side_out(uses, target, group):
                act.wait_ge(s_side_full, uses + group + 1)
                if group in (V0, V1):
                    vh = group - V0
                    if not (isinstance(target, int) and target == 0):
                        act.wait_ge(s_load_v[1], 16 * target)
                    act.activation(v_new[:, :, 4 * vh : 4 * vh + 4, 0:D], side[:].rearrange("p (t n d) -> p n t d", t=4, n=2),
                                   ACT.Copy).then_inc(s_vhi, 1)
                    return
                of = target % CT if isinstance(target, int) else target & 3
                column = ds((PAIRS if group >= K0 else 0) + of, 1)
                act.wait_ge(s_qklo, 4 * target + group + 1)
                act.sem_inc(s_passed["act"], 1)
                act.activation(qk_full[group % 2][:], side[:], ACT.Identity, bias=qk_bias[:, column],
                               scale=qk_scale[:, column]).then_inc(s_qkfull, 1)
                act.wait_ge(s_qkfull, 4 * target + group + 1)
                act.sem_inc(s_side_free, 1)
                if group == Q0 and not (isinstance(target, int) and target == 0):
                    act.wait_ge(s_load_a[1], 64 * target)
                    act.wait_ge(s_load_b[1], 32 * target)
                cols = slice((group % 2) * HALF, (group % 2 + 1) * HALF)
                act.activation(qk[:, 0, group // K0, cols], qk_full[group % 2][:], ACT.Copy).then_inc(s_qkhi, 1)

            def projected(uses, t, qh):
                act.wait_ge(s_side_full, uses + qh + 1)
                act.wait_ge(s_out[qh], 16 + 16 * (t - PAIRS))
                act.sem_inc(s_passed["act"], 1)
                r = 3 * CT + (t % CT if isinstance(t, int) else t & 3)
                act.activation(y_tile[qh][:], side[:], ACT.Identity, bias=bias[:, ds(r, 1)], scale=row_scale[:, ds(r, 1)]).then_inc(s_y, 1)
                act.wait_ge(s_y, 2 * (t - PAIRS) + qh + 1)
                act.sem_inc(s_side_free, 1)

            def exponentials(t, par, j):
                g = 2 * t + par
                u = UNITS * g + j
                act.wait_ge(s_full[j % 2], UNITS // 2 * g + j // 2 + 1)
                act.wait_ge(s_plo, u + 1)
                act.wait_ge(s_keysum, u + 1)
                act.activation(prob[j % 4], score[j % 2][:], ACT.Exp, bias=exp_bias[:, 0:1], scale=SCALE).then_inc(s_exp, 1)
                act.wait_ge(s_exp, u + 1)
                act.sem_inc(s_free[j % 2], 1)
                act.wait_ge(s_pfree, u + 1)
                act.activation(p_hi[j % 4], prob[j % 4], ACT.Copy).then_inc(s_phi, 1)

            def key_high(g, qh):
                act.wait_ge(s_acc, 2 * g + qh + 1)
                act.wait_ge(s_z, g + 1)
                act.activation(key_parts[qh][:, 0, :], key_sums[qh][:], ACT.Copy).then_inc(s_keyhi, 1)

            def max_rows(g, par):
                act.wait_ge(s_mrow, g + 1)
                act.activation(q_b[par][D : D + 2, :], maxes[0:2, :], ACT.Copy).then_inc(s_mrows, 1)

            def output(g, qh):
                act.wait_ge(s_pfree, 4 + 4 * (2 * g + qh + 1))
                act.wait_ge(s_oshift[qh], 32 * g + 32)
                act.activation(o_raw[qh][:], pv[:], ACT.Copy).then_inc(s_oraw, 1)

            def denominators(g, par):
                act.wait_ge(s_invrow, g + 1)
                if par == 0:
                    act.wait_ge(s_omul, g // 2 + 1 if isinstance(g, int) else (g >> 1) + 1)
                r = slice(D * par, D * par + D)
                act.activation(denom[r, :], maxes[r, :], ACT.Copy, scale=1.0 / INV_SCALE).then_inc(s_denom, 1)

            def output_high(q):
                act.wait_ge(s_omul, 1 + q + 1)
                act.sem_inc(s_passed["act"], 1)
                act.activation(o_hi[:, slot_of(q), :].rearrange("p a l -> p (a l)"), o_sum, ACT.Copy).then_inc(s_ohi, 1)

            for group in range(6):
                side_out(0, 0, group)
            max_rows(0, 0)

            def pair(t, before, after, qkv, norm, proj):
                for par in range(2):
                    g = 2 * t + par
                    previous = before or par == 1
                    following = after or par == 0
                    for j in range(UNITS):
                        exponentials(t, par, j)
                        if j == 1 and previous:
                            output(g - 1, 1)
                        if j == 0 and previous:
                            key_high(g - 1, 1)
                        if j == 2 and previous:
                            denominators(g - 1, 1 - par)
                        if j == 4:
                            key_high(g, 0)
                        if par == 1 and j == 4 and norm:
                            normed_high(t + CT + 1)
                        if j == 5:
                            output(g, 0)
                        if par == 0 and j == 5 and before:
                            output_high(t - 1)
                        if j == UNITS - 1 and following:
                            max_rows(g + 1, 1 - par)
                        group = (UNITS * par + j) // 2
                        if j % 2 == 1:
                            if group < O0 and qkv:
                                side_out(side_uses(t), t + 1, group)
                            if group >= O0 and proj:
                                projected(proj_uses(t, qkv), t, group - O0)

            def flush():
                g = HEADS * B - 1
                key_high(g, 1)
                output(g, 1)
                denominators(g, 1)
                output_high(T - 1)
                with act.Fori(0, CT) as c:
                    for qh in range(2):
                        projected(LAST_USES + 2 * c, T + c, qh)

            steps(act, pair, flush)

        @block.vector
        def _(dve):
            chain = [0]

            def link(ins):
                chain[0] += 1
                ins.then_inc(s_setup_v, 1)
                dve.wait_ge(s_setup_v, chain[0])

            dve.sem_inc(s_plo, 4)
            dve.sem_inc(s_qklo, 2)
            dve.sem_inc(s_yx, 2)
            link(dve.memset(ones[:], 1.0))
            dve.sem_inc(s_keylo, 2)
            link(dve.memset(exp_bias[:], P_SHIFT))
            link(dve.memset(minus_half[:], -0.5))
            for par in range(2):
                link(dve.memset(k_b[par][D : D + 2, :], M_SCALE))
            dve.wait_ge(s_setup_in, 16 * 6)
            dve.tensor_copy(ident16[:], ident[:]).then_inc(s_consts, 1)
            dve.wait_ge(s_w_in, 48)

            def fold(t, bias_row, scale_row):
                link(dve.tensor_tensor_reduce(denom[:, 0:C], w_row(t), rows[:, bias_row, :], 1.0, 0.0,
                                              ALU.mult, ALU.add, bias_w[:, t : t + 1]))
                link(dve.tensor_tensor(w_row(t), w_row(t), rows[:, scale_row, :], ALU.mult))
                link(dve.tensor_reduce(row_max[:, t : t + 1], w_row(t), AX_X, ALU.max, apply_absolute_value=True))

            def scale_rows(t0, t1, with_bias):
                r = slice(t0, t1)
                link(dve.tensor_tensor(bias[:, r], bias_w[:, r], bias_in[:, r], ALU.add))
                if with_bias:
                    link(dve.tensor_scalar(bias_abs[:, r], bias[:, r], -1.0, None, ALU.mult))
                    link(dve.tensor_tensor(bias_abs[:, r], bias_abs[:, r], bias[:, r], ALU.max))
                    link(dve.tensor_tensor(row_max[:, r], row_max[:, r], bias_abs[:, r], ALU.max))
                link(dve.tensor_scalar(row_scale[:, r], row_max[:, r], TINY, None, ALU.max))
                link(dve.reciprocal(row_inv[:, r], row_scale[:, r]))

            def low_rows(t):
                dve.wait_ge(s_whi, t + 1)
                dve.tensor_tensor(w_lo[:, :, t * P : (t + 1) * P], score[t % 2][:, 0, :].rearrange("p (c r) -> p c r", c=CT),
                                  w_hi[:, :, t * P : (t + 1) * P], ALU.subtract).then_inc(s_wlo, 1)

            def split_rows(t0, t1):
                for t in range(t0, t1):
                    dve.tensor_scalar(w_row(t), w_row(t), row_inv[:, t : t + 1], None, ALU.mult).then_inc(s_wrow, 1)
                    if t > t0:
                        low_rows(t - 1)
                low_rows(t1 - 1)

            for t in range(3 * CT):
                fold(t, NORM_B, NORM_W)
            scale_rows(0, 2 * CT, True)
            scale_rows(2 * CT, 3 * CT, False)
            dve.sem_inc(s_vscale, 1)
            link(dve.tensor_tensor(qk_scale[:, 0:PAIRS], row_scale[:, 0:PAIRS], row_scale[:, PAIRS : 2 * PAIRS], ALU.mult))
            link(dve.memset(qk_scale[:, PAIRS:], 1.0))
            link(dve.tensor_tensor(qk_bias[:, 0:PAIRS], bias[:, 0:PAIRS], row_scale[:, PAIRS : 2 * PAIRS], ALU.mult))
            link(dve.tensor_tensor(qk_bias[:, PAIRS:], bias[:, PAIRS : 2 * PAIRS], row_inv[:, PAIRS : 2 * PAIRS], ALU.mult))
            split_rows(0, 3 * CT)
            dve.wait_ge(s_vscale_in, 32)
            for t in range(3 * CT, RT):
                fold(t, V_BIAS, V_SCALE)
            scale_rows(3 * CT, RT, False)
            split_rows(3 * CT, RT)

            def statistics(m):
                dve.wait_ge(s_xn, 16 * (m + 1))
                for half in range(2):
                    dve.bn_stats(stats[:, half, :], x_norm[:, half * HALF : (half + 1) * HALF]).then_inc(s_bn, 1)
                dve.wait_ge(s_bn, 2 * (m + 1))
                dve.sem_inc(s_passed["dve"], 1)
                dve.bn_aggr(mean_var[:], stats[:].rearrange("p a s -> p (a s)")).then_inc(s_stats, 1)

            def spreads(m):
                dve.wait_ge(s_gmean, m + 1)
                dve.tensor_copy(g_mean[:], maxes[:, 16:17]).then_inc(s_dve, 1)
                dve.wait_ge(s_dve, 3 * m + 1)
                dve.tensor_tensor(dev[:], mean_var[:, 0:1], g_mean[:], ALU.subtract).then_inc(s_dve, 1)
                dve.wait_ge(s_dve, 3 * m + 2)
                dve.tensor_tensor(dev2[:], dev[:], dev[:], ALU.mult).then_inc(s_dve, 1)
                dve.wait_ge(s_dve, 3 * m + 3)
                dve.tensor_tensor(spread[:], dev2[:], mean_var[:, 1:2], ALU.add).then_inc(s_spread, 1)

            def variance(m):
                dve.wait_ge(s_gvar, m + 1)
                dve.tensor_scalar(var_eps[:], maxes[:, 17:18], EPS, None, ALU.add).then_inc(s_vareps, 1)

            def normalise(m):
                dve.wait_ge(s_rstd, m + 1)
                dve.tensor_scalar(x_norm[:], x_norm[:], g_mean[:], rstd[:], ALU.subtract, ALU.mult).then_inc(s_xnorm, 1)

            for m in range(CT + 1):
                statistics(m)
                spreads(m)
                variance(m)
                normalise(m)

            def side_low(target, group):
                if group in (V0, V1):
                    vh = group - V0
                    new = v_new[:, :, 4 * vh : 4 * vh + 4, :]
                    dve.wait_ge(s_vhi, 2 * target + vh + 1)
                    dve.tensor_tensor(new[:, :, :, D : 2 * D], side[:].rearrange("p (t n d) -> p n t d", t=4, n=2),
                                      new[:, :, :, 0:D], ALU.subtract).then_inc(s_vlo, 1)
                    dve.wait_ge(s_vlo, 2 * target + vh + 1)
                    dve.sem_inc(s_side_free, 1)
                    return
                cols = slice((group % 2) * HALF, (group % 2 + 1) * HALF)
                hi, lo = (qk[:, part, group // K0, cols] for part in range(2))
                if group == Q0 and not (isinstance(target, int) and target == 0):
                    dve.wait_ge(s_load_a[1], 64 * target)
                    dve.wait_ge(s_load_b[1], 32 * target)
                dve.wait_ge(s_qkhi, 4 * target + group + 1)
                dve.tensor_tensor(lo, qk_full[group % 2][:], hi, ALU.subtract).then_inc(s_qklo, 1)

            def add_residual(t, qh):
                dve.wait_ge(s_y, 2 * (t - PAIRS) + qh + 1)
                dve.wait_ge(s_res[qh], 16 * (t - PAIRS) + 16)
                dve.tensor_tensor(y_tile[qh][:], y_tile[qh][:], x_res[qh][:], ALU.add).then_inc(s_yx, 1)

            def reduce_max(g, par, t):
                dve.wait_ge(s_max, LT * g + t + 1)
                dve.tensor_reduce(neg_max[par][:, t : t + 1], maxes[:], AX_X, ALU.max, negate=True).then_inc(s_maxed, 1)
                if t == LT - 1:
                    dve.wait_ge(s_maxed, LT * (g + 1))
                    dve.tensor_scalar(neg_max_scaled[:], neg_max[par][:], 1.0 / M_SCALE, None, ALU.mult).then_inc(s_mscaled, 1)
                    dve.wait_ge(s_mscaled, g + 1)
                    dve.tensor_copy(neg_max_parts[par][:, :, 0], neg_max_scaled[:]).then_inc(s_mhi, 1)
                    dve.wait_ge(s_mhi, g + 1)
                    dve.tensor_tensor(neg_max_parts[par][:, :, 1], neg_max_scaled[:], neg_max_parts[par][:, :, 0],
                                      ALU.subtract).then_inc(s_mcols, 1)

            def low_probabilities(u, j):
                dve.wait_ge(s_phi, u + 1)
                dve.wait_ge(s_pfree, u + 1)
                dve.tensor_tensor(p_lo[j % 4], prob[j % 4], p_hi[j % 4], ALU.subtract).then_inc(s_plo, 1)

            def key_low(g, qh):
                dve.wait_ge(s_keyhi, 2 * g + qh + 1)
                dve.tensor_tensor(key_parts[qh][:, 1, :], key_sums[qh][:], key_parts[qh][:, 0, :], ALU.subtract).then_inc(s_keylo, 1)

            def inverses(g):
                dve.wait_ge(s_z, 1 + g + 1)
                dve.reciprocal(inv[:], maxes[:, 8 : 8 + LT]).then_inc(s_inv, 1)
                dve.wait_ge(s_inv, g + 1)
                dve.tensor_scalar(inv_scaled[:], inv[:], INV_SCALE, None, ALU.mult).then_inc(s_inv_scaled, 1)
                dve.wait_ge(s_inv_scaled, g + 1)
                dve.tensor_copy(inv_parts[:, 0, :], inv_scaled[:]).then_inc(s_invhi, 1)
                dve.wait_ge(s_invhi, g + 1)
                dve.tensor_tensor(inv_parts[:, 1, :], inv_scaled[:], inv_parts[:, 0, :], ALU.subtract).then_inc(s_invparts, 1)

            for group in range(6):
                side_low(0, group)
            for t in range(LT):
                reduce_max(0, 0, t)

            def pair(t, before, after, qkv, norm, proj):
                for par in range(2):
                    g = 2 * t + par
                    previous = before or par == 1
                    following = after or par == 0
                    for j in range(UNITS):
                        if norm and par == 1 and j == 0:
                            spreads(t + CT + 1)
                        if norm and par == 1 and j == 1:
                            variance(t + CT + 1)
                        if following and j in EARLY_TILE:
                            reduce_max(g + 1, 1 - par, EARLY_TILE[j])
                        low_probabilities(UNITS * g + j, j)
                        if j == 0 and previous:
                            key_low(g - 1, 1)
                        if j == 1 and previous:
                            inverses(g - 1)
                        if following and j in LATE_TILE:
                            reduce_max(g + 1, 1 - par, LATE_TILE[j])
                        if j == 4:
                            key_low(g, 0)
                        group = (UNITS * par + j) // 2
                        if j % 2 == 1:
                            if group < O0 and qkv:
                                side_low(t + 1, group)
                            if group >= O0 and proj:
                                add_residual(t, group - O0)
                        if norm and par == 0 and j == 1:
                            statistics(t + CT + 1)
                        if norm and par == 1 and j == 3:
                            normalise(t + CT + 1)

            def flush():
                key_low(HEADS * B - 1, 1)
                inverses(HEADS * B - 1)
                with dve.Fori(T, T + PAIRS) as t:
                    for qh in range(2):
                        add_residual(t, qh)

            steps(dve, pair, flush)

        @block.gpsimd
        def _(pool):
            pool.sem_inc(s_pfree, 4)
            pool.sem_inc(s_z, 1)
            pool.sem_inc(s_keysum, 4)
            for i in range(2):
                pool.sem_inc(s_oshift[i], 32)
                pool.sem_inc(s_out[i], 16)
            pool.sem_inc(s_omul, 1)
            pool.sem_inc(s_ohi, 1)
            pool.sem_inc(s_olo, 1)

            def slot_of(m):
                return ds(m % (2 * CT) if isinstance(m, int) else m & (2 * CT - 1), 1)

            def inverse_spread(m):
                pool.wait_ge(s_vareps, m + 1)
                pool.tensor_tensor(rstd[:], var_eps[:], minus_half[:], ALU.pow).then_inc(s_rstd, 1)

            def normed_low(m):
                pool.wait_ge(s_hhi, m + 1)
                hi, lo = (h[:, slot_of(m), :].rearrange("p a l -> p (a l)") for h in (h_hi, h_lo))
                pool.tensor_tensor(lo, x_norm[:], hi, ALU.subtract).then_inc(s_hlo, 1)

            pool.wait_ge(s_setup_v, 3)
            for m in range(CT + 1):
                inverse_spread(m)
                normed_low(m)

            ADDS = 7

            def add_keys(g, par, j):
                i, kp = divmod(j, 4)
                w = 2 * g + i
                acc, pr = key_sums[i], prob[j % 4]
                pool.wait_ge(s_exp, UNITS * g + j + 1)
                if kp == 0:
                    pool.wait_ge(s_keylo, 2 * g + i + 1)
                    pool.tensor_tensor(acc[:], pr[:, 0, :], pr[:, 1, :], ALU.add).then_inc(s_pool, 1)
                    pool.wait_ge(s_pool, ADDS * w + 1)
                else:
                    for k in range(2):
                        pool.tensor_tensor(acc[:], acc[:], pr[:, k, :], ALU.add).then_inc(s_pool, 1)
                        pool.wait_ge(s_pool, ADDS * w + 2 * kp + k)
                pool.sem_inc(s_keysum, 1)
                if kp == 3:
                    pool.sem_inc(s_acc, 1)

            def merge(q):
                for qh in range(2):
                    pool.wait_ge(s_oshift[qh], 32 + 64 * (q + 1))
                pool.tensor_tensor(o_sum, o_sum, o_part, ALU.add).then_inc(s_oadd, 1)

            def divide(q):
                pool.wait_ge(s_oadd, q + 1)
                pool.wait_ge(s_denom, 2 * (q + 1))
                pool.tensor_tensor(o_sum, o_sum, denom[:], ALU.mult).then_inc(s_omul, 1)

            def output_low(q):
                pool.wait_ge(s_ohi, 1 + q + 1)
                hi, lo = (o[:, slot_of(q), :].rearrange("p a l -> p (a l)") for o in (o_hi, o_lo))
                pool.tensor_tensor(lo, o_sum, hi, ALU.subtract).then_inc(s_olo, 1)

            def pair(t, before, after, qkv, norm, proj):
                for par in range(2):
                    g = 2 * t + par
                    for j in range(UNITS):
                        add_keys(g, par, j)
                        if par == 0 and before:
                            if j == 3:
                                merge(t - 1)
                            if j == 4:
                                divide(t - 1)
                            if j == 6:
                                output_low(t - 1)
                        if par == 1 and norm:
                            if j == 1:
                                inverse_spread(t + CT + 1)
                            if j == 5:
                                normed_low(t + CT + 1)

            def flush():
                merge(T - 1)
                divide(T - 1)
                output_low(T - 1)

            steps(pool, pair, flush)


_INS = ["x", "L0_conv_norm_w", "L0_conv_norm_b", "L0_conv_qkv_w", "L0_conv_qkv_b", "L0_conv_proj_w", "L0_conv_proj_b"]


def kernel(**inputs):
    import numpy as _np
    import concourse.bacc as _bacc
    from concourse import mybir as _mybir
    from concourse.bass_utils import run_bass_kernel_spmd as _run

    nc = _bacc.Bacc("TRN2", target_bir_lowering=False, num_devices=1)
    arrays, args = {}, []
    channels_per_group = inputs["x"].shape[1] // GROUPS
    constants = {
        "identity": _np.eye(P, dtype=_np.float32),
        "group_average": _np.kron(_np.eye(P // channels_per_group), _np.full((channels_per_group,) * 2, 1.0 / channels_per_group)).astype(_np.float32),
    }
    for name in _INS + list(constants):
        a = _np.ascontiguousarray(inputs[name] if name in inputs else constants[name])
        arrays[f"in_{name}"] = a
        args.append(nc.dram_tensor(f"in_{name}", a.shape, _mybir.dt.from_np(a.dtype), kind="ExternalInput").ap())
    y = nc.dram_tensor("out_y", inputs["x"].shape, _mybir.dt.float32, kind="ExternalOutput").ap()
    build_attention_block(nc, *args, y)
    r = _run(nc, [arrays], core_ids=[0])
    return r.results[0]["out_y"]
```

```python
from contextlib import ExitStack

import numpy as np

import concourse.bass as bass
from concourse import mybir

ALU = mybir.AluOpType
ACT = mybir.ActivationFunctionType
AX_X = mybir.AxisListType.X
F32 = mybir.dt.float32
F16 = mybir.dt.float16

P = 128
GROUPS = 32
EPS = 1e-5
TINY = 1e-30
P_SHIFT = 6.0 * float(np.log(2.0))
M_SCALE = 64.0
INV_SCALE = 4096.0


def ds(start, size):
    return bass.ds(start, size)


def build_attention_block(nc, x, norm_w, norm_b, qkv_w, qkv_b, proj_w, proj_b, ident_in, group_in, out):
    B, C, H, W = x.shape
    L = H * W
    HEADS = 8
    D = C // HEADS
    CT = C // P
    LT = L // P
    PAIRS = HEADS // 2
    T = B * PAIRS
    HALF = L // 2
    UNITS = LT
    ROWS = 3 * C + C
    RT = ROWS // P
    SCALE = float(D) ** -0.5
    assert D == 64 and HALF == 512 and CT == 4 and LT == 8 and PAIRS == CT

    Q0, Q1, K0, K1, V0, V1, O0, O1 = range(8)

    def side_uses(t):
        return 6 + 6 * t if isinstance(t, int) and t < PAIRS else 8 * t - 2

    EARLY_TILE = {3: 1, 4: 3, 5: 5, 6: 7}
    LATE_TILE = {2: 0, 3: 2, 4: 4, 5: 6}

    x_tiles = x.rearrange("b (t p) h w -> (b t) p (h w)", p=P)
    out_tiles = out.rearrange("b (t p) h w -> (b t) p (h w)", p=P)
    value_rows = nc.dram_tensor("value_rows", [2, C], F32, kind="Internal").ap()

    with ExitStack() as ctx:

        def sb(name, shape, dt=F32):
            return ctx.enter_context(nc.sbuf_tensor(name, shape, dt))

        def sem(name):
            return ctx.enter_context(nc.semaphore(name))

        def sems(name):
            return [sem(f"{name}{i}") for i in range(2)]

        w_hi = sb("w_hi", [P, CT, ROWS], F16)
        w_lo = sb("w_lo", [P, CT, ROWS], F16)
        h_hi = sb("h_hi", [P, 2 * CT, L], F16)
        h_lo = sb("h_lo", [P, 2 * CT, L], F16)
        o_hi = sb("o_hi", [P, 2 * PAIRS, L], F16)
        o_lo = sb("o_lo", [P, 2 * PAIRS, L], F16)
        x_norm = sb("x_norm", [P, L])
        x_res = [sb(f"x_res{i}", [P, HALF]) for i in range(2)]
        y_tile = [sb(f"y_tile{i}", [P, HALF]) for i in range(2)]
        qk_full = [sb(f"qk_full{i}", [P, HALF]) for i in range(2)]
        qk = sb("qk", [P, 2, 2, L], F16)
        v_new = sb("v_new", [P, 2, LT, 2 * D], F16)
        q_a = [sb(f"q_a{i}", [P, L], F16) for i in range(2)]
        q_b = [sb(f"q_b{i}", [P, L], F16) for i in range(2)]
        k_a = [sb(f"k_a{i}", [P, L], F16) for i in range(2)]
        k_b = [sb(f"k_b{i}", [P, L], F16) for i in range(2)]
        v_head = [sb(f"v_head{i}", [P, LT, 2 * D], F16) for i in range(2)]
        prob_all = sb("prob_all", [P, 4, 2, HALF])
        p_parts = sb("p_parts", [P, 2, 4, 2, HALF], F16)
        prob = [prob_all[:, i] for i in range(4)]
        p_hi = [p_parts[:, 0, i] for i in range(4)]
        p_lo = [p_parts[:, 1, i] for i in range(4)]
        key_sums = [sb(f"key_sums{i}", [P, HALF]) for i in range(2)]
        key_parts = [sb(f"key_parts{i}", [P, 2, HALF], F16) for i in range(2)]
        o_raw = [sb(f"o_raw{i}", [P, HALF]) for i in range(2)]
        o_pair = sb("o_pair", [P, 2, L])
        o_sum, o_part = o_pair[:, 0, :], o_pair[:, 1, :]
        denom = sb("denom", [P, L])
        ident = sb("ident", [P, P])
        ident16 = sb("ident16", [P, P], F16)
        group_mean = sb("group_mean", [P, P])
        ones = sb("ones", [P, 1], F16)
        neg_max = [sb(f"neg_max{i}", [P, LT]) for i in range(2)]
        neg_max_scaled = sb("neg_max_scaled", [P, LT])
        neg_max_parts = [sb(f"neg_max_parts{i}", [P, LT, 2], F16) for i in range(2)]
        inv = sb("inv", [P, LT])
        inv_scaled = sb("inv_scaled", [P, LT])
        inv_parts = sb("inv_parts", [P, 2, LT], F16)
        exp_bias = sb("exp_bias", [P, 1])
        bias_w = sb("bias_w", [P, RT])
        bias_in = sb("bias_in", [P, RT])
        bias = sb("bias", [P, RT])
        row_max = sb("row_max", [P, RT])
        row_scale = sb("row_scale", [P, RT])
        row_inv = sb("row_inv", [P, RT])
        bias_abs = sb("bias_abs", [P, RT])
        qk_scale = sb("qk_scale", [P, 2 * PAIRS])
        qk_bias = sb("qk_bias", [P, 2 * PAIRS])
        stats = sb("stats", [P, CT + 1, 2, 6])
        mean_var = sb("mean_var", [P, CT + 1, 2])
        g_mean = sb("g_mean", [P, CT + 1])
        dev = sb("dev", [P, CT + 1])
        dev2 = sb("dev2", [P, CT + 1])
        spread = sb("spread", [P, CT + 1])
        var_eps = sb("var_eps", [P, CT + 1])
        rstd = sb("rstd", [P, CT + 1])
        minus_half = sb("minus_half", [P, CT + 1])

        row_homes = (prob_all[:].rearrange("p a b l -> p (a b l)"),
                     p_parts[:].rearrange("p a b c l -> p (a b c l)").bitcast(F32))

        def w_row(t):
            return row_homes[t // 8][:, (t % 8) * C : (t % 8 + 1) * C]

        def w_rows(t):
            return row_homes[t // 8][:, (t % 8) * C : (t % 8 + 4) * C].rearrange("p (t c) -> p t c", c=C)

        def x_home(m):
            home = (o_hi, o_lo)[m // CT][:, 2 * (m % CT) : 2 * (m % CT) + 2, :]
            return home.rearrange("p a l -> p (a l)").bitcast(F32)

        rows = o_pair[:].rearrange("p a l -> p (a l)").rearrange("p (r c) -> p r c", r=4)
        NORM_W, NORM_B, V_BIAS, V_SCALE = range(4)

        score = [ctx.enter_context(nc.psum_tensor(f"score{i}", [P, 2, HALF], F32)) for i in range(2)]
        maxes = ctx.enter_context(nc.psum_tensor("maxes", [P, L], F32))
        pv = ctx.enter_context(nc.psum_tensor("pv", [P, HALF], F32))
        side = ctx.enter_context(nc.psum_tensor("side", [P, HALF], F32))

        max_banks = [maxes[:]] + [score[i][:].rearrange("p a l -> p (a l)") for i in range(2)]

        turns = (side[:], pv[:])

        s_setup_in = sem("s_setup_in")
        s_w_in = [sem(f"s_w_in_{name}") for name in ("q", "k", "v", "proj")]
        s_consts = sem("s_consts")
        s_setup_v = sem("s_setup_v")
        s_vscale = sem("s_vscale")
        s_vscale_out = sem("s_vscale_out")
        s_vscale_in = sem("s_vscale_in")
        s_wrow = sem("s_wrow")
        s_wt = sem("s_wt")
        s_whi = sem("s_whi")
        s_wlo = sem("s_wlo")
        s_xn = sem("s_xn")
        s_bn = sem("s_bn")
        s_stats = sem("s_stats")
        s_gmean = sem("s_gmean")
        s_dve = sem("s_dve")
        s_spread = sem("s_spread")
        s_gvar = sem("s_gvar")
        s_vareps = sem("s_vareps")
        s_rstd = sem("s_rstd")
        s_xnorm = sem("s_xnorm")
        s_hhi = sem("s_hhi")
        s_hlo = sem("s_hlo")
        s_side_full = sem("s_side_full")
        s_side_free = sem("s_side_free")
        s_qkfull = sem("s_qkfull")
        s_qkhi = sem("s_qkhi")
        s_qklo = sem("s_qklo")
        s_vhi = sem("s_vhi")
        s_vlo = sem("s_vlo")
        s_res = sems("s_res")
        s_y = sem("s_y")
        s_yx = sem("s_yx")
        s_out = sems("s_out")
        s_load_a = sems("s_load_a")
        s_load_b = sems("s_load_b")
        s_load_v = sems("s_load_v")
        s_full = sems("s_full")
        s_free = sems("s_free")
        s_max = sem("s_max")
        s_maxed = sem("s_maxed")
        s_mscaled = sem("s_mscaled")
        s_mhi = sem("s_mhi")
        s_mcols = sem("s_mcols")
        s_mrow = sem("s_mrow")
        s_mrows = sem("s_mrows")
        s_exp = sem("s_exp")
        s_phi = sem("s_phi")
        s_plo = sem("s_plo")
        s_pfree = sem("s_pfree")
        s_keysum = sem("s_keysum")
        s_pool = sem("s_pool")
        s_acc = sem("s_acc")
        s_keyhi = sem("s_keyhi")
        s_keylo = sem("s_keylo")
        s_z = sem("s_z")
        s_inv = sem("s_inv")
        s_inv_scaled = sem("s_inv_scaled")
        s_invhi = sem("s_invhi")
        s_invparts = sem("s_invparts")
        s_invrow = sem("s_invrow")
        s_denom = sem("s_denom")
        s_oraw = sem("s_oraw")
        s_oshift = sems("s_oshift")
        s_oadd = sem("s_oadd")
        s_omul = sem("s_omul")
        s_ohi = sem("s_ohi")
        s_olo = sem("s_olo")
        s_passed = {name: sem(f"s_passed_{name}") for name in ("sp", "pe", "act", "dve")}

        block = ctx.enter_context(nc.Block())

        def steps(eng, pair, flush):
            pair(0, before=False, after=True, qkv=True, norm=True, proj=False)
            for t in range(1, PAIRS):
                pair(t, before=True, after=True, qkv=True, norm=True, proj=False)
            with eng.Fori(PAIRS, T - PAIRS - 1) as t:
                pair(t, before=True, after=True, qkv=True, norm=True, proj=True)
            with eng.Fori(T - PAIRS - 1, T - 1) as t:
                pair(t, before=True, after=True, qkv=True, norm=False, proj=True)
            pair(T - 1, before=True, after=False, qkv=False, norm=False, proj=True)
            flush()

        def proj_uses(t, after_qkv):
            return side_uses(t) + (6 if after_qkv else 0)

        LAST_USES = side_uses(T - 1) + 2

        @block.sync
        def _(sp):
            def wait_passed(semaphore, value):
                sp.wait_ge(semaphore, value)
                sp.sem_inc(s_passed["sp"], 1)

            sp.dma_start(rows[:, NORM_W, :], norm_w.rearrange("(a c) -> a c", a=1).to_broadcast([P, C])).then_inc(s_setup_in, 16)
            sp.dma_start(rows[:, NORM_B, :], norm_b.rearrange("(a c) -> a c", a=1).to_broadcast([P, C])).then_inc(s_setup_in, 16)
            with nc.allow_non_contiguous_dma(reason="biases, once"):
                sp.dma_start(bias_in[:, 0 : RT - CT], qkv_b.rearrange("(t p) -> p t", p=P)).then_inc(s_setup_in, 16)
                sp.dma_start(bias_in[:, RT - CT : RT], proj_b.rearrange("(t p) -> p t", p=P)).then_inc(s_setup_in, 16)
            sp.dma_start(ident[:], ident_in).then_inc(s_setup_in, 16)
            sp.dma_start(group_mean[:], group_in).then_inc(s_setup_in, 16)
            for m in range(CT + 1):
                sp.dma_start(x_home(m), x_tiles[m, :, :]).then_inc(s_xn, 16)
            qkv_rows = qkv_w.rearrange("(t p) c -> p t c", p=P)
            for part in (2, 0, 1):
                sp.dma_start(w_rows(CT * part), qkv_rows[:, CT * part : CT * (part + 1), :]).then_inc(s_w_in[part], 16)
            sp.dma_start(w_rows(3 * CT), proj_w.rearrange("(t p) c -> p t c", p=P)).then_inc(s_w_in[3], 16)
            sp.wait_ge(s_vscale, 1)
            with nc.allow_non_contiguous_dma(reason="scales and biases, once"):
                sp.dma_start(value_rows[0, :].rearrange("(t p) -> p t", p=P), row_scale[:, 2 * CT : 3 * CT]).then_inc(s_vscale_out, 16)
                sp.dma_start(value_rows[1, :].rearrange("(t p) -> p t", p=P), bias[:, 2 * CT : 3 * CT]).then_inc(s_vscale_out, 16)
            sp.wait_ge(s_vscale_out, 32)
            sp.dma_start(rows[:, V_SCALE, :], value_rows[0:1, :].to_broadcast([P, C])).then_inc(s_vscale_in, 16)
            sp.dma_start(rows[:, V_BIAS, :], value_rows[1:2, :].to_broadcast([P, C])).then_inc(s_vscale_in, 16)

            def load_x(m):
                sp.dma_start(x_norm[:], x_tiles[ds(m, 1), :, :].rearrange("a p l -> p (a l)")).then_inc(s_xn, 16)

            def load_scores(par):
                r = slice(D * par, D * par + D)
                sp.dma_start(q_a[par][0:D, :], qk[r, 0, 0, :]).then_inc(s_load_a[par], 16)
                sp.dma_start(k_a[par][0:D, :], qk[r, 0, 1, :]).then_inc(s_load_a[par], 16)
                sp.dma_start(q_a[par][D:P, :], qk[r, 1, 0, :]).then_inc(s_load_a[par], 16)
                sp.dma_start(k_a[par][D:P, :], qk[r, 0, 1, :]).then_inc(s_load_a[par], 16)
                sp.dma_start(q_b[par][0:D, :], qk[r, 0, 0, :]).then_inc(s_load_b[par], 16)
                sp.dma_start(k_b[par][0:D, :], qk[r, 1, 1, :]).then_inc(s_load_b[par], 16)

            def load_values(par):
                sp.dma_start(v_head[par][:], v_new[:, par, :, :]).then_inc(s_load_v[par], 16)

            def shift(g, par):
                r = slice(D * par, D * par + D)
                for qh in range(2):
                    wait_passed(s_oraw, 2 * g + qh + 1)
                    cols = slice(qh * HALF, (qh + 1) * HALF)
                    sp.dma_start(o_sum[r, cols], o_raw[qh][0:D, :]).then_inc(s_oshift[qh], 16)
                    sp.dma_start(o_part[r, cols], o_raw[qh][D:P, :]).then_inc(s_oshift[qh], 16)

            def load_residual(t):
                wait_passed(s_yx, 2 + 2 * (t - PAIRS))
                for qh in range(2):
                    sp.dma_start(x_res[qh][:], x_tiles[ds(t - PAIRS, 1), :, qh * HALF : (qh + 1) * HALF].rearrange("a p l -> p (a l)")).then_inc(s_res[qh], 16)

            def store(t):
                for qh in range(2):
                    wait_passed(s_yx, 2 + 2 * (t - PAIRS) + qh + 1)
                    sp.dma_start(out_tiles[ds(t - PAIRS, 1), :, qh * HALF : (qh + 1) * HALF].rearrange("a p l -> p (a l)"), y_tile[qh][:]).then_inc(s_out[qh], 16)

            wait_passed(s_qklo, 2 + 4)
            load_scores(0)
            load_scores(1)
            wait_passed(s_vlo, 2)
            load_values(0)

            def pair(t, before, after, qkv, norm, proj):
                g = 2 * t
                if norm:
                    wait_passed(s_hlo, t + CT + 1)
                    load_x(t + CT + 1)
                if before:
                    wait_passed(s_pfree, 4 + UNITS * g)
                load_values(1)
                if proj:
                    load_residual(t)
                if before:
                    shift(g - 1, 1)
                if after:
                    wait_passed(s_qklo, 2 + 4 * (t + 2))
                    wait_passed(s_exp, UNITS * (g + 1))
                    load_scores(0)
                wait_passed(s_olo, t + 1)
                wait_passed(s_ohi, t + 1)
                shift(g, 0)
                if after:
                    wait_passed(s_vlo, 2 * (t + 2))
                    wait_passed(s_pfree, 4 + UNITS * (g + 1))
                    load_values(0)
                    wait_passed(s_exp, UNITS * (g + 2))
                    load_scores(1)
                if proj:
                    store(t)

            def flush():
                shift(HEADS * B - 1, 1)
                with sp.Fori(T, T + PAIRS) as t:
                    load_residual(t)
                    store(t)

            steps(sp, pair, flush)
            for i in range(2):
                sp.wait_ge(s_out[i], 16 + 16 * T)

        @block.tensor
        def _(pe):
            pe.wait_ge(s_setup_in, 16 * 6)

            def group_product(m, n=1):
                pe.wait_ge(s_stats, m + n)
                pe.matmul(maxes[:, 16 : 16 + n], group_mean[:], mean_var[:, 0:n, 0], start=True, stop=True).then_inc(s_gmean, n)

            def group_spread(m, n=1):
                pe.wait_ge(s_spread, m + n)
                pe.matmul(maxes[:, 24 : 24 + n], group_mean[:], spread[:, 0:n], start=True, stop=True).then_inc(s_gvar, n)

            group_product(0, CT + 1)
            group_spread(0, CT + 1)
            pe.wait_ge(s_vareps, CT + 1)

            for t in range(RT):
                pe.wait_ge(s_wrow, t + 1)
                if t >= 2:
                    pe.wait_ge(s_wlo, t - 1)
                for c in range(CT):
                    mm = pe.transpose(score[t % 2][:, 0, c * P : (c + 1) * P], w_row(t)[:, c * P : (c + 1) * P], ident[:])
                mm.then_inc(s_wt, 1)
            pe.wait_ge(s_wlo, RT)
            pe.wait_ge(s_consts, 1)


            def half_of_products(w0, rhs_hi, rhs_lo, slot, qh, part, bank):
                cols = slice(qh * HALF, (qh + 1) * HALF)
                for c in range(2 * part, 2 * part + 2):
                    r_hi, r_lo = (r[:, ds(slot + c, 1), cols].rearrange("p a l -> p (a l)") for r in (rhs_hi, rhs_lo))
                    pe.matmul(bank, w_hi[:, c, ds(w0, P)], r_hi, start=(c == 0), stop=False)
                    pe.matmul(bank, w_hi[:, c, ds(w0, P)], r_lo, start=False, stop=False)
                    mm = pe.matmul(bank, w_lo[:, c, ds(w0, P)], r_hi, start=False, stop=(c == CT - 1))
                return mm

            def value_products(pair_of, slot, vh, part, bank):
                for lt in range(4 * vh + 2 * part, 4 * vh + 2 * part + 2):
                    dst = bank[:, (lt % 4) * P : (lt % 4 + 1) * P]
                    for c in range(CT):
                        hh, hl = (h[:, ds(slot + c, 1), lt * P : (lt + 1) * P].rearrange("p a l -> p (a l)") for h in (h_hi, h_lo))
                        wh, wl = (w[:, c, ds(2 * C + P * pair_of, P)] for w in (w_hi, w_lo))
                        pe.matmul(dst, hh, wh, start=(c == 0), stop=False)
                        pe.matmul(dst, hh, wl, start=False, stop=False)
                        mm = pe.matmul(dst, hl, wh, start=False, stop=(c == CT - 1))
                return mm

            def side_product(uses, target, group, part, bank=side[:], banks=1):
                if part == 0:
                    free = uses + group + 2 - banks
                    pe.wait_ge(s_side_free, max(free, 1) if isinstance(free, int) else free)
                slot = CT * ((target // CT) % 2) if isinstance(target, int) else CT * ((target >> 2) & 1)
                of = target % CT if isinstance(target, int) else target & 3
                if group in (V0, V1):
                    mm = value_products(of, slot, group - V0, part, bank)
                elif group in (O0, O1):
                    mm = half_of_products(3 * C + P * of, o_hi, o_lo, slot, group - O0, part, bank)
                else:
                    mm = half_of_products((C if group >= K0 else 0) + P * of, h_hi, h_lo, slot, group % 2, part, bank)
                if part == 1:
                    mm.then_inc(s_side_full, 1)

            def max_tile(g, par, t, bank=maxes[:], banks=1):
                if t == 0:
                    pe.wait_ge(s_load_a[par], 64 * (g // 2 + 1) if isinstance(g, int) else 64 * (g >> 1) + 64)
                if t >= banks:
                    pe.wait_ge(s_maxed, LT * g + t + 1 - banks)
                for half in range(2):
                    mm = pe.matmul(bank[:, half * HALF : (half + 1) * HALF], q_a[par][:, t * P : (t + 1) * P],
                                   k_a[par][:, half * HALF : (half + 1) * HALF], start=True, stop=True)
                mm.then_inc(s_max, 1)

            def max_rows(g, par):
                pe.wait_ge(s_mcols, g + 1)
                for t in range(LT):
                    mm = pe.matmul(maxes[0:2, t * P : (t + 1) * P], neg_max_parts[par][:, t, :], ident16[:], start=True, stop=True)
                mm.then_inc(s_mrow, 1)

            def scores(t, par, j):
                g = 2 * t + par
                qh, kp = divmod(j, 4)
                if j == 0:
                    pe.wait_ge(s_load_b[par], 32 * (t + 1))
                    pe.wait_ge(s_mrows, g + 1)
                pe.wait_ge(s_free[j % 2], UNITS // 2 * g + j // 2 + 1)
                cols = slice(qh * HALF, (qh + 1) * HALF)
                for i in range(2):
                    keys = slice((2 * kp + i) * P, (2 * kp + i + 1) * P)
                    pe.matmul(score[j % 2][:, i, :], k_a[par][:, keys], q_a[par][:, cols], start=True, stop=False)
                    mm = pe.matmul(score[j % 2][:, i, :], k_b[par][0 : D + 2, keys], q_b[par][0 : D + 2, cols], start=False, stop=True)
                mm.then_inc(s_full[j % 2], 1)

            def values(g, par, j):
                kp = j % 4
                if j == 0:
                    pe.wait_ge(s_load_v[par], 16 * (g // 2 + 1) if isinstance(g, int) else 16 * (g >> 1) + 16)
                if kp == 0 and not (isinstance(g, int) and g == 0 and j == 0):
                    pe.wait_ge(s_oraw, 2 * g + j // 4)
                pe.wait_ge(s_plo, 4 + UNITS * g + j + 1)
                for i in range(2):
                    v = v_head[par][:, 2 * kp + i, :]
                    pe.matmul(pv[:], v, p_hi[j % 4][:, i, :], start=(kp == 0 and i == 0), stop=False)
                    mm = pe.matmul(pv[:], v, p_lo[j % 4][:, i, :], start=False, stop=(kp == 3 and i == 1))
                mm.then_inc(s_pfree, 1)

            def softmax_sums(g):
                pe.wait_ge(s_keylo, 2 + 2 * (g + 1))
                for t in range(LT):
                    for part in range(2):
                        mm = pe.matmul(maxes[:, 8 + t : 9 + t], key_parts[t // 4][:, part, (t % 4) * P : (t % 4 + 1) * P], ones[:],
                                       start=(part == 0), stop=(part == 1))
                mm.then_inc(s_z, 1)

            def inverse_rows(g):
                pe.wait_ge(s_invparts, g + 1)
                for t in range(LT):
                    for part in range(2):
                        mm = pe.matmul(maxes[:, t * P : (t + 1) * P], inv_parts[:, part, t : t + 1].to_broadcast([P, P]), ident16[:],
                                       start=(part == 0), stop=(part == 1))
                mm.then_inc(s_invrow, 1)

            pe.wait_ge(s_hlo, CT)
            for group in range(6):
                for part in range(2):
                    side_product(0, 0, group, part, turns[group % 2], 2)
            pe.wait_ge(s_hlo, CT + 1)
            for t in range(LT):
                max_tile(0, 0, t, max_banks[t % 3], 3)
            max_rows(0, 0)

            def pair(t, before, after, qkv, norm, proj):
                for par in range(2):
                    g = 2 * t + par
                    previous = before or par == 1
                    following = after or par == 0
                    for j in range(UNITS):
                        if j == 0:
                            if previous:
                                values(g - 1, 1 - par, UNITS - 2)
                            scores(t, par, j)
                            if norm and par == 1:
                                group_product(t + CT + 1)
                        else:
                            if norm and par == 1 and j == 1:
                                group_spread(t + CT + 1)
                            scores(t, par, j)
                            if j >= 2:
                                values(g, par, j - 2)
                            elif previous:
                                values(g - 1, 1 - par, UNITS - 1)
                        if j == 2 and previous:
                            inverse_rows(g - 1)
                        if j == UNITS - 1 and following:
                            max_rows(g + 1, 1 - par)
                        group = (UNITS * par + j) // 2
                        if following and j in EARLY_TILE:
                            max_tile(g + 1, 1 - par, EARLY_TILE[j])
                        if group in (Q0, V0) and j == 0 and qkv:
                            pe.wait_ge(s_hlo, CT * ((t + 1) >> 2) + CT)
                            pe.sem_inc(s_passed["pe"], 1)
                        if group < O0 and qkv:
                            side_product(side_uses(t), t + 1, group, j % 2)
                        if group >= O0 and proj:
                            if group == O0 and j % 2 == 0:
                                pe.wait_ge(s_olo, 1 + t)
                                pe.wait_ge(s_ohi, 1 + t)
                            side_projection(t, group, j % 2, qkv)
                        if following and j in LATE_TILE:
                            if LATE_TILE[j] == 0 and previous:
                                pe.wait_ge(s_denom, g)
                            max_tile(g + 1, 1 - par, LATE_TILE[j])
                        if j == 1 and previous:
                            if norm and par == 1:
                                pe.wait_ge(s_vareps, t + CT + 2)
                            softmax_sums(g - 1)

            def side_projection(t, group, part, after_qkv):
                uses = proj_uses(t, after_qkv) - O0
                side_product(uses, t - PAIRS, group, part)

            def flush():
                g = HEADS * B - 1
                for j in range(2):
                    values(g, 1, UNITS - 2 + j)
                softmax_sums(g)
                inverse_rows(g)
                pe.wait_ge(s_olo, 1 + T)
                pe.wait_ge(s_ohi, 1 + T)
                with pe.Fori(0, CT) as c:
                    for group in (O0, O1):
                        for part in range(2):
                            side_product(LAST_USES + 2 * c - O0, T - PAIRS + c, group, part, turns[group % 2], 2)

            steps(pe, pair, flush)

        @block.scalar
        def _(act):
            for i in range(2):
                act.sem_inc(s_free[i], 1)
            act.sem_inc(s_side_free, 1)
            def slot_of(m):
                return ds(m % (2 * CT) if isinstance(m, int) else m & (2 * CT - 1), 1)

            def normed_high(m, x_tile):
                act.wait_ge(s_xnorm, m + 1)
                act.sem_inc(s_passed["act"], 1)
                act.activation(h_hi[:, slot_of(m), :].rearrange("p a l -> p (a l)"), x_tile, ACT.Copy).then_inc(s_hhi, 1)

            for m in range(CT + 1):
                normed_high(m, x_home(m))
            for t in range(RT):
                act.wait_ge(s_wt, t + 1)
                act.activation(w_hi[:, :, t * P : (t + 1) * P], score[t % 2][:, 0, :].rearrange("p (c r) -> p c r", c=CT),
                               ACT.Copy).then_inc(s_whi, 1)

            def side_out(uses, target, group, bank=side[:]):
                act.wait_ge(s_side_full, uses + group + 1)
                if group in (V0, V1):
                    vh = group - V0
                    if not (isinstance(target, int) and target == 0):
                        act.wait_ge(s_load_v[1], 16 * target)
                    act.activation(v_new[:, :, 4 * vh : 4 * vh + 4, 0:D], bank.rearrange("p (t n d) -> p n t d", t=4, n=2),
                                   ACT.Copy).then_inc(s_vhi, 1)
                    return
                of = target % CT if isinstance(target, int) else target & 3
                column = ds((PAIRS if group >= K0 else 0) + of, 1)
                act.wait_ge(s_qklo, 4 * target + group + 1)
                act.sem_inc(s_passed["act"], 1)
                act.activation(qk_full[group % 2][:], bank, ACT.Identity, bias=qk_bias[:, column],
                               scale=qk_scale[:, column]).then_inc(s_qkfull, 1)
                act.wait_ge(s_qkfull, 4 * target + group + 1)
                act.sem_inc(s_side_free, 1)
                if group == Q0 and not (isinstance(target, int) and target == 0):
                    act.wait_ge(s_load_a[1], 64 * target)
                    act.wait_ge(s_load_b[1], 32 * target)
                cols = slice((group % 2) * HALF, (group % 2 + 1) * HALF)
                act.activation(qk[:, 0, group // K0, cols], qk_full[group % 2][:], ACT.Copy).then_inc(s_qkhi, 1)

            def projected(uses, t, qh, bank=side[:]):
                act.wait_ge(s_side_full, uses + qh + 1)
                act.wait_ge(s_out[qh], 16 + 16 * (t - PAIRS))
                act.sem_inc(s_passed["act"], 1)
                r = 3 * CT + (t % CT if isinstance(t, int) else t & 3)
                act.activation(y_tile[qh][:], bank, ACT.Identity, bias=bias[:, ds(r, 1)], scale=row_scale[:, ds(r, 1)]).then_inc(s_y, 1)
                act.wait_ge(s_y, 2 * (t - PAIRS) + qh + 1)
                act.sem_inc(s_side_free, 1)

            def exponentials(t, par, j, previous):
                g = 2 * t + par
                u = UNITS * g + j
                act.wait_ge(s_full[j % 2], UNITS // 2 * g + j // 2 + 1)
                act.wait_ge(s_plo, u + 1)
                act.wait_ge(s_keysum, u + 1)
                act.activation(prob[j % 4], score[j % 2][:], ACT.Exp, bias=exp_bias[:, 0:1], scale=SCALE).then_inc(s_exp, 1)
                act.wait_ge(s_exp, u + 1)
                act.sem_inc(s_free[j % 2], 1)
                if j == 2 and previous:
                    denominators(g - 1, 1 - par)
                act.wait_ge(s_pfree, u + 1)
                act.activation(p_hi[j % 4], prob[j % 4], ACT.Copy).then_inc(s_phi, 1)

            def key_high(g, qh):
                act.wait_ge(s_acc, 2 * g + qh + 1)
                act.wait_ge(s_z, g + 1)
                act.activation(key_parts[qh][:, 0, :], key_sums[qh][:], ACT.Copy).then_inc(s_keyhi, 1)

            def max_rows(g, par):
                act.wait_ge(s_mrow, g + 1)
                act.activation(q_b[par][D : D + 2, :], maxes[0:2, :], ACT.Copy).then_inc(s_mrows, 1)

            def output(g, qh):
                act.wait_ge(s_pfree, 4 + 4 * (2 * g + qh + 1))
                act.wait_ge(s_oshift[qh], 32 * g + 32)
                act.activation(o_raw[qh][:], pv[:], ACT.Copy).then_inc(s_oraw, 1)

            def denominators(g, par):
                act.wait_ge(s_invrow, g + 1)
                if par == 0:
                    act.wait_ge(s_omul, g // 2 + 1 if isinstance(g, int) else (g >> 1) + 1)
                r = slice(D * par, D * par + D)
                act.activation(denom[r, :], maxes[r, :], ACT.Copy, scale=1.0 / INV_SCALE).then_inc(s_denom, 1)

            def output_high(q):
                act.wait_ge(s_omul, 1 + q + 1)
                act.sem_inc(s_passed["act"], 1)
                act.activation(o_hi[:, slot_of(q), :].rearrange("p a l -> p (a l)"), o_sum, ACT.Copy).then_inc(s_ohi, 1)

            for group in range(6):
                side_out(0, 0, group, turns[group % 2])
            max_rows(0, 0)

            def pair(t, before, after, qkv, norm, proj):
                for par in range(2):
                    g = 2 * t + par
                    previous = before or par == 1
                    following = after or par == 0
                    for j in range(UNITS):
                        exponentials(t, par, j, previous)
                        if j == 1 and previous:
                            output(g - 1, 1)
                        if j == 0 and previous:
                            key_high(g - 1, 1)
                        if j == 4:
                            key_high(g, 0)
                        if par == 1 and j == 4 and norm:
                            normed_high(t + CT + 1, x_norm[:])
                        if j == 5:
                            output(g, 0)
                        if par == 0 and j == 5 and before:
                            output_high(t - 1)
                        if j == UNITS - 1 and following:
                            max_rows(g + 1, 1 - par)
                        group = (UNITS * par + j) // 2
                        if j % 2 == 1:
                            if group < O0 and qkv:
                                side_out(side_uses(t), t + 1, group)
                            if group >= O0 and proj:
                                projected(proj_uses(t, qkv), t, group - O0)

            def flush():
                g = HEADS * B - 1
                key_high(g, 1)
                output(g, 1)
                denominators(g, 1)
                output_high(T - 1)
                with act.Fori(0, CT) as c:
                    for qh in range(2):
                        projected(LAST_USES + 2 * c, T + c, qh, turns[qh])

            steps(act, pair, flush)

        @block.vector
        def _(dve):
            chain = [0]

            def link(ins):
                chain[0] += 1
                ins.then_inc(s_setup_v, 1)
                dve.wait_ge(s_setup_v, chain[0])

            dve.sem_inc(s_plo, 4)
            dve.sem_inc(s_qklo, 2)
            dve.sem_inc(s_yx, 2)
            link(dve.memset(ones[:], 1.0))
            dve.sem_inc(s_keylo, 2)
            link(dve.memset(exp_bias[:], P_SHIFT))
            link(dve.memset(minus_half[:], -0.5))
            for par in range(2):
                link(dve.memset(k_b[par][D : D + 2, :], M_SCALE))
            dve.wait_ge(s_setup_in, 16 * 6)
            dve.tensor_copy(ident16[:], ident[:]).then_inc(s_consts, 1)

            def statistics(m, x_tiles_in):
                n = len(x_tiles_in)
                dve.wait_ge(s_xn, 16 * (m + n))
                for i, x_tile in enumerate(x_tiles_in):
                    for half in range(2):
                        dve.bn_stats(stats[:, i, half, :], x_tile[:, half * HALF : (half + 1) * HALF]).then_inc(s_bn, 1)
                dve.wait_ge(s_bn, 2 * (m + n))
                dve.sem_inc(s_passed["dve"], 1)
                for i in range(n):
                    dve.bn_aggr(mean_var[:, i, :], stats[:, i, :, :].rearrange("p a s -> p (a s)")).then_inc(s_stats, 1)

            def spreads(m, n=1):
                dve.wait_ge(s_gmean, m + n)
                dve.tensor_copy(g_mean[:, 0:n], maxes[:, 16 : 16 + n]).then_inc(s_dve, n)
                dve.wait_ge(s_dve, 3 * m + n)
                dve.tensor_tensor(dev[:, 0:n], mean_var[:, 0:n, 0], g_mean[:, 0:n], ALU.subtract).then_inc(s_dve, n)
                dve.wait_ge(s_dve, 3 * m + 2 * n)
                dve.tensor_tensor(dev2[:, 0:n], dev[:, 0:n], dev[:, 0:n], ALU.mult).then_inc(s_dve, n)
                dve.wait_ge(s_dve, 3 * m + 3 * n)
                dve.tensor_tensor(spread[:, 0:n], dev2[:, 0:n], mean_var[:, 0:n, 1], ALU.add).then_inc(s_spread, n)

            def variance(m, n=1):
                dve.wait_ge(s_gvar, m + n)
                dve.tensor_scalar(var_eps[:, 0:n], maxes[:, 24 : 24 + n], EPS, None, ALU.add).then_inc(s_vareps, n)

            def normalise(m, x_tile, i):
                dve.wait_ge(s_rstd, m + 1)
                dve.tensor_scalar(x_tile, x_tile, g_mean[:, i : i + 1], rstd[:, i : i + 1], ALU.subtract, ALU.mult).then_inc(s_xnorm, 1)

            fold_scratch = (denom[:, 0:C], denom[:, C : 2 * C], o_raw[0][:], o_raw[1][:])

            def fold_bias(t, bias_row):
                link(dve.tensor_tensor_reduce(fold_scratch[t % 4], w_row(t), rows[:, bias_row, :], 1.0, 0.0,
                                              ALU.mult, ALU.add, bias_w[:, t : t + 1]))

            def fold_scale(t, scale_row):
                scale = rows[:, scale_row : scale_row + 1, :].to_broadcast([P, 4, C])
                link(dve.tensor_tensor(w_rows(t), w_rows(t), scale, ALU.mult))
                link(dve.tensor_reduce(row_max[:, t : t + 4], w_rows(t), AX_X, ALU.max, apply_absolute_value=True))

            def fold(part):
                dve.wait_ge(s_w_in[part], 16)
                for t in range(CT * part, CT * (part + 1)):
                    fold_bias(t, NORM_B)
                fold_scale(CT * part, NORM_W)

            def scale_rows(t0, t1, with_bias):
                r = slice(t0, t1)
                link(dve.tensor_tensor(bias[:, r], bias_w[:, r], bias_in[:, r], ALU.add))
                if with_bias:
                    link(dve.tensor_scalar(bias_abs[:, r], bias[:, r], -1.0, None, ALU.mult))
                    link(dve.tensor_tensor(bias_abs[:, r], bias_abs[:, r], bias[:, r], ALU.max))
                    link(dve.tensor_tensor(row_max[:, r], row_max[:, r], bias_abs[:, r], ALU.max))
                link(dve.tensor_scalar(row_scale[:, r], row_max[:, r], TINY, None, ALU.max))
                link(dve.reciprocal(row_inv[:, r], row_scale[:, r]))

            def scaled_rows(t):
                dve.tensor_scalar(w_row(t), w_row(t), row_inv[:, t : t + 1], None, ALU.mult).then_inc(s_wrow, 1)

            def low_rows(t):
                dve.wait_ge(s_whi, t + 1)
                dve.tensor_tensor(w_lo[:, :, t * P : (t + 1) * P], score[t % 2][:, 0, :].rearrange("p (c r) -> p c r", c=CT),
                                  w_hi[:, :, t * P : (t + 1) * P], ALU.subtract).then_inc(s_wlo, 1)

            statistics(0, [x_home(m) for m in range(CT + 1)])
            fold(2)
            scale_rows(2 * CT, 3 * CT, False)
            dve.sem_inc(s_vscale, 1)
            spreads(0, CT + 1)
            fold(0)
            variance(0, CT + 1)
            fold(1)
            for m in range(CT + 1):
                normalise(m, x_home(m), m)
            scale_rows(0, 2 * CT, True)
            link(dve.tensor_tensor(qk_scale[:, 0:PAIRS], row_scale[:, 0:PAIRS], row_scale[:, PAIRS : 2 * PAIRS], ALU.mult))
            link(dve.memset(qk_scale[:, PAIRS:], 1.0))
            link(dve.tensor_tensor(qk_bias[:, 0:PAIRS], bias[:, 0:PAIRS], row_scale[:, PAIRS : 2 * PAIRS], ALU.mult))
            link(dve.tensor_tensor(qk_bias[:, PAIRS:], bias[:, PAIRS : 2 * PAIRS], row_inv[:, PAIRS : 2 * PAIRS], ALU.mult))
            for t in range(2):
                scaled_rows(t)
            for t in range(RT):
                if t + 2 < RT:
                    scaled_rows(t + 2)
                low_rows(t)
                if t == 4:
                    dve.wait_ge(s_vscale_in, 32)
                    dve.wait_ge(s_w_in[3], 16)
                if 4 <= t < 8:
                    fold_bias(3 * CT + t - 4, V_BIAS)
                if t == 8:
                    fold_scale(3 * CT, V_SCALE)
                    scale_rows(3 * CT, RT, False)

            def side_low(target, group, bank=side[:]):
                if group in (V0, V1):
                    vh = group - V0
                    new = v_new[:, :, 4 * vh : 4 * vh + 4, :]
                    dve.wait_ge(s_vhi, 2 * target + vh + 1)
                    dve.tensor_tensor(new[:, :, :, D : 2 * D], bank.rearrange("p (t n d) -> p n t d", t=4, n=2),
                                      new[:, :, :, 0:D], ALU.subtract).then_inc(s_vlo, 1)
                    dve.wait_ge(s_vlo, 2 * target + vh + 1)
                    dve.sem_inc(s_side_free, 1)
                    return
                cols = slice((group % 2) * HALF, (group % 2 + 1) * HALF)
                hi, lo = (qk[:, part, group // K0, cols] for part in range(2))
                if group == Q0 and not (isinstance(target, int) and target == 0):
                    dve.wait_ge(s_load_a[1], 64 * target)
                    dve.wait_ge(s_load_b[1], 32 * target)
                dve.wait_ge(s_qkhi, 4 * target + group + 1)
                dve.tensor_tensor(lo, qk_full[group % 2][:], hi, ALU.subtract).then_inc(s_qklo, 1)

            def add_residual(t, qh):
                dve.wait_ge(s_y, 2 * (t - PAIRS) + qh + 1)
                dve.wait_ge(s_res[qh], 16 * (t - PAIRS) + 16)
                dve.tensor_tensor(y_tile[qh][:], y_tile[qh][:], x_res[qh][:], ALU.add).then_inc(s_yx, 1)

            def reduce_max(g, par, t, bank=maxes[:]):
                dve.wait_ge(s_max, LT * g + t + 1)
                dve.tensor_reduce(neg_max[par][:, t : t + 1], bank, AX_X, ALU.max, negate=True).then_inc(s_maxed, 1)
                if t == LT - 1:
                    dve.wait_ge(s_maxed, LT * (g + 1))
                    dve.tensor_scalar(neg_max_scaled[:], neg_max[par][:], 1.0 / M_SCALE, None, ALU.mult).then_inc(s_mscaled, 1)
                    dve.wait_ge(s_mscaled, g + 1)
                    dve.tensor_copy(neg_max_parts[par][:, :, 0], neg_max_scaled[:]).then_inc(s_mhi, 1)
                    dve.wait_ge(s_mhi, g + 1)
                    dve.tensor_tensor(neg_max_parts[par][:, :, 1], neg_max_scaled[:], neg_max_parts[par][:, :, 0],
                                      ALU.subtract).then_inc(s_mcols, 1)

            def low_probabilities(u, j):
                dve.wait_ge(s_phi, u + 1)
                dve.wait_ge(s_pfree, u + 1)
                dve.tensor_tensor(p_lo[j % 4], prob[j % 4], p_hi[j % 4], ALU.subtract).then_inc(s_plo, 1)

            def key_low(g, qh):
                dve.wait_ge(s_keyhi, 2 * g + qh + 1)
                dve.tensor_tensor(key_parts[qh][:, 1, :], key_sums[qh][:], key_parts[qh][:, 0, :], ALU.subtract).then_inc(s_keylo, 1)

            def inverses(g):
                dve.wait_ge(s_z, 1 + g + 1)
                dve.reciprocal(inv[:], maxes[:, 8 : 8 + LT]).then_inc(s_inv, 1)
                dve.wait_ge(s_inv, g + 1)
                dve.tensor_scalar(inv_scaled[:], inv[:], INV_SCALE, None, ALU.mult).then_inc(s_inv_scaled, 1)
                dve.wait_ge(s_inv_scaled, g + 1)
                dve.tensor_copy(inv_parts[:, 0, :], inv_scaled[:]).then_inc(s_invhi, 1)
                dve.wait_ge(s_invhi, g + 1)
                dve.tensor_tensor(inv_parts[:, 1, :], inv_scaled[:], inv_parts[:, 0, :], ALU.subtract).then_inc(s_invparts, 1)

            for group in range(6):
                side_low(0, group, turns[group % 2])
            for t in range(LT):
                reduce_max(0, 0, t, max_banks[t % 3])

            def pair(t, before, after, qkv, norm, proj):
                for par in range(2):
                    g = 2 * t + par
                    previous = before or par == 1
                    following = after or par == 0
                    for j in range(UNITS):
                        if norm and par == 1 and j == 0:
                            spreads(t + CT + 1)
                        if norm and par == 1 and j == 1:
                            variance(t + CT + 1)
                        if following and j in EARLY_TILE:
                            reduce_max(g + 1, 1 - par, EARLY_TILE[j])
                        if j == 1 and previous:
                            inverses(g - 1)
                        if j == 2 and following:
                            reduce_max(g + 1, 1 - par, LATE_TILE[j])
                        low_probabilities(UNITS * g + j, j)
                        if j == 0 and previous:
                            key_low(g - 1, 1)
                        group = (UNITS * par + j) // 2
                        if following and j in LATE_TILE and j != 2:
                            reduce_max(g + 1, 1 - par, LATE_TILE[j])
                        if j == 4:
                            key_low(g, 0)
                        if j % 2 == 1:
                            if group < O0 and qkv:
                                side_low(t + 1, group)
                            if group >= O0 and proj:
                                add_residual(t, group - O0)
                        if norm and par == 0 and j == 1:
                            statistics(t + CT + 1, [x_norm[:]])
                        if norm and par == 1 and j == 3:
                            normalise(t + CT + 1, x_norm[:], 0)

            def flush():
                key_low(HEADS * B - 1, 1)
                inverses(HEADS * B - 1)
                with dve.Fori(T, T + PAIRS) as t:
                    for qh in range(2):
                        add_residual(t, qh)

            steps(dve, pair, flush)

        @block.gpsimd
        def _(pool):
            pool.sem_inc(s_pfree, 4)
            pool.sem_inc(s_z, 1)
            pool.sem_inc(s_keysum, 4)
            for i in range(2):
                pool.sem_inc(s_oshift[i], 32)
                pool.sem_inc(s_out[i], 16)
            pool.sem_inc(s_omul, 1)
            pool.sem_inc(s_ohi, 1)
            pool.sem_inc(s_olo, 1)

            def slot_of(m):
                return ds(m % (2 * CT) if isinstance(m, int) else m & (2 * CT - 1), 1)

            def inverse_spread(m, n=1):
                pool.wait_ge(s_vareps, m + n)
                pool.tensor_tensor(rstd[:, 0:n], var_eps[:, 0:n], minus_half[:, 0:n], ALU.pow).then_inc(s_rstd, n)

            def normed_low(m, x_tile):
                pool.wait_ge(s_hhi, m + 1)
                hi, lo = (h[:, slot_of(m), :].rearrange("p a l -> p (a l)") for h in (h_hi, h_lo))
                pool.tensor_tensor(lo, x_tile, hi, ALU.subtract).then_inc(s_hlo, 1)

            pool.wait_ge(s_setup_v, 3)
            inverse_spread(0, CT + 1)
            for m in range(CT + 1):
                normed_low(m, x_home(m))

            ADDS = 7

            def add_keys(g, par, j):
                i, kp = divmod(j, 4)
                w = 2 * g + i
                acc, pr = key_sums[i], prob[j % 4]
                pool.wait_ge(s_exp, UNITS * g + j + 1)
                if kp == 0:
                    pool.wait_ge(s_keylo, 2 * g + i + 1)
                    pool.tensor_tensor(acc[:], pr[:, 0, :], pr[:, 1, :], ALU.add).then_inc(s_pool, 1)
                    pool.wait_ge(s_pool, ADDS * w + 1)
                else:
                    for k in range(2):
                        pool.tensor_tensor(acc[:], acc[:], pr[:, k, :], ALU.add).then_inc(s_pool, 1)
                        pool.wait_ge(s_pool, ADDS * w + 2 * kp + k)
                pool.sem_inc(s_keysum, 1)
                if kp == 3:
                    pool.sem_inc(s_acc, 1)

            def merge(q):
                for qh in range(2):
                    pool.wait_ge(s_oshift[qh], 32 + 64 * (q + 1))
                pool.tensor_tensor(o_sum, o_sum, o_part, ALU.add).then_inc(s_oadd, 1)

            def divide(q):
                pool.wait_ge(s_oadd, q + 1)
                pool.wait_ge(s_denom, 2 * (q + 1))
                pool.tensor_tensor(o_sum, o_sum, denom[:], ALU.mult).then_inc(s_omul, 1)

            def output_low(q):
                pool.wait_ge(s_ohi, 1 + q + 1)
                hi, lo = (o[:, slot_of(q), :].rearrange("p a l -> p (a l)") for o in (o_hi, o_lo))
                pool.tensor_tensor(lo, o_sum, hi, ALU.subtract).then_inc(s_olo, 1)

            def pair(t, before, after, qkv, norm, proj):
                for par in range(2):
                    g = 2 * t + par
                    for j in range(UNITS):
                        add_keys(g, par, j)
                        if par == 0 and before:
                            if j == 3:
                                merge(t - 1)
                            if j == 4:
                                divide(t - 1)
                            if j == 6:
                                output_low(t - 1)
                        if par == 1 and norm:
                            if j == 1:
                                inverse_spread(t + CT + 1)
                            if j == 5:
                                normed_low(t + CT + 1, x_norm[:])

            def flush():
                merge(T - 1)
                divide(T - 1)
                output_low(T - 1)

            steps(pool, pair, flush)


_INS = ["x", "L0_conv_norm_w", "L0_conv_norm_b", "L0_conv_qkv_w", "L0_conv_qkv_b", "L0_conv_proj_w", "L0_conv_proj_b"]


def kernel(**inputs):
    import numpy as _np
    import concourse.bacc as _bacc
    from concourse import mybir as _mybir
    from concourse.bass_utils import run_bass_kernel_spmd as _run

    nc = _bacc.Bacc("TRN2", target_bir_lowering=False, num_devices=1)
    arrays, args = {}, []
    channels_per_group = inputs["x"].shape[1] // GROUPS
    constants = {
        "identity": _np.eye(P, dtype=_np.float32),
        "group_average": _np.kron(_np.eye(P // channels_per_group), _np.full((channels_per_group,) * 2, 1.0 / channels_per_group)).astype(_np.float32),
    }
    for name in _INS + list(constants):
        a = _np.ascontiguousarray(inputs[name] if name in inputs else constants[name])
        arrays[f"in_{name}"] = a
        args.append(nc.dram_tensor(f"in_{name}", a.shape, _mybir.dt.from_np(a.dtype), kind="ExternalInput").ap())
    y = nc.dram_tensor("out_y", inputs["x"].shape, _mybir.dt.float32, kind="ExternalOutput").ap()
    build_attention_block(nc, *args, y)
    r = _run(nc, [arrays], core_ids=[0])
    return r.results[0]["out_y"]
```
